# Optimizing a Trainium2 kernel written in Bass

```python
import numpy as np
import jax
import jax.numpy as jnp

def _softmax(x, axis=-1):
    return jax.nn.softmax(x, axis=axis)

def _gelu(x):
    return jax.nn.gelu(x, approximate=True)

def _silu(x):
    return jax.nn.silu(x)

def _sigmoid(x):
    return jax.nn.sigmoid(x)

def _layernorm(x, axis=-1, eps=1e-05):
    m = jnp.mean(x, axis=axis, keepdims=True)
    v = jnp.var(x, axis=axis, keepdims=True)
    return (x - m) / jnp.sqrt(v + eps)

def _scatter_add(tgt, idx, src, axis=0):
    return tgt.at[idx].add(src)

def _segment_sum(src, seg, n):
    return jax.ops.segment_sum(src, seg, n)
kernel_name = 'mk_seq_postln_d1_jaxref_r4_0397bf'

def setup_inputs(seed: int=0):
    np.random.seed(seed)
    _w = jnp.asarray

    def _L0_attn_setup():
        import jax, jax.numpy as jnp
        import numpy as np
        EMBED = 256
        HEADS = 16
        HEAD_DIM = EMBED // HEADS
        B, T = (2, 512)
        ROPE_THETA = 10000.0

        def _rope(x):
            D = x.shape[-1]
            inv_freq = 1.0 / ROPE_THETA ** (jnp.arange(0, D, 2, dtype=jnp.float32) / D)
            freqs = jnp.arange(x.shape[2], dtype=jnp.float32)[:, None] * inv_freq[None, :]
            cos = jnp.cos(freqs).astype(x.dtype)
            sin = jnp.sin(freqs).astype(x.dtype)
            x1, x2 = (x[..., :D // 2], x[..., D // 2:])
            return jnp.concatenate([x1 * cos - x2 * sin, x2 * cos + x1 * sin], axis=-1)
        key = jax.random.key(seed)
        ks = jax.random.split(key, 5)
        s = 1.0 / np.sqrt(EMBED)
        return {'x': jax.random.normal(ks[0], (B, T, EMBED), dtype=jnp.float32), 'Wq': jax.random.normal(ks[1], (EMBED, EMBED), dtype=jnp.float32) * s, 'bq': jnp.zeros((EMBED,), dtype=jnp.float32), 'Wk': jax.random.normal(ks[2], (EMBED, EMBED), dtype=jnp.float32) * s, 'bk': jnp.zeros((EMBED,), dtype=jnp.float32), 'Wv': jax.random.normal(ks[3], (EMBED, EMBED), dtype=jnp.float32) * s, 'bv': jnp.zeros((EMBED,), dtype=jnp.float32), 'Wo': jax.random.normal(ks[4], (EMBED, EMBED), dtype=jnp.float32) * s, 'bo': jnp.zeros((EMBED,), dtype=jnp.float32)}
    _L0_attn_in = _L0_attn_setup()

    def _L0_ffn_setup():
        import jax, jax.numpy as jnp
        import numpy as np
        H, HP, NH_M, NH_D = (256, 64, 8, 8)
        B, T = (2, 512)
        SPARSITY = 8
        N_ROT = 32
        BASE = 10000.0

        def _rope(x, pos, n_rot, base):
            half = n_rot // 2
            inv = base ** (-jnp.arange(half, dtype=x.dtype) / half)
            ang = pos[..., None] * inv
            cos, sin = (jnp.cos(ang), jnp.sin(ang))
            x1, x2 = (x[..., :half], x[..., half:n_rot])
            rot = jnp.concatenate([x1 * cos - x2 * sin, x1 * sin + x2 * cos], axis=-1)
            return jnp.concatenate([rot, x[..., n_rot:]], axis=-1)

        def _mosa_branch(X, router_w, wqkv, wo):
            b, t, _ = X.shape
            k = t // SPARSITY
            scores = jnp.einsum('bth,hn->bnt', X, router_w)
            _, idx = jax.lax.top_k(scores, k)
            idx = jnp.sort(idx, axis=-1)
            gates = jax.nn.sigmoid(jnp.take_along_axis(scores, idx, axis=-1))
            Xg = jnp.take_along_axis(X[:, None], idx[..., None], axis=2)
            qkv = jnp.einsum('bnkh,hnd->bnkd', Xg, wqkv)
            Q, K, V = jnp.split(qkv, 3, axis=-1)
            pos = idx.astype(X.dtype)
            Q = _rope(Q, pos, N_ROT, BASE)
            K = _rope(K, pos, N_ROT, BASE)
            att = jnp.einsum('bnqd,bnkd->bnqk', Q, K) / jnp.sqrt(jnp.asarray(HP, X.dtype))
            causal = idx[..., :, None] >= idx[..., None, :]
            att = jnp.where(causal, att, -jnp.inf)
            AV = jnp.einsum('bnqk,bnkd->bnqd', jax.nn.softmax(att, axis=-1), V)
            AV = AV * gates[..., None]
            out = jnp.zeros((b, NH_M, t, HP), X.dtype)
            bi = jnp.arange(b)[:, None, None]
            hi = jnp.arange(NH_M)[None, :, None]
            out = out.at[bi, hi, idx].set(AV)
            out = out.transpose(0, 2, 1, 3).reshape(b, t, NH_M * HP)
            return out @ wo

        def _dense_branch(X, wqkv, wo):
            b, t, _ = X.shape
            qkv = jnp.einsum('bth,hnd->bntd', X, wqkv)
            Q, K, V = jnp.split(qkv, 3, axis=-1)
            pos = jnp.arange(t, dtype=X.dtype)
            Q = _rope(Q, pos, N_ROT, BASE)
            K = _rope(K, pos, N_ROT, BASE)
            att = jnp.einsum('bnqd,bnkd->bnqk', Q, K) / jnp.sqrt(jnp.asarray(HP, X.dtype))
            causal = jnp.tril(jnp.ones((t, t), bool))
            att = jnp.where(causal, att, -jnp.inf)
            AV = jnp.einsum('bnqk,bnkd->bnqd', jax.nn.softmax(att, axis=-1), V)
            return AV.transpose(0, 2, 1, 3).reshape(b, t, NH_D * HP) @ wo
        key = jax.random.key(seed)
        ks = jax.random.split(key, 6)
        s = 0.02
        return {'X': jax.random.normal(ks[0], (B, T, H), jnp.float32), 'mosa_router_w': jax.random.normal(ks[1], (H, NH_M), jnp.float32) * s, 'mosa_wqkv': jax.random.normal(ks[2], (H, NH_M, 3 * HP), jnp.float32) * s, 'mosa_wo': jax.random.normal(ks[3], (NH_M * HP, H), jnp.float32) * s, 'dense_wqkv': jax.random.normal(ks[4], (H, NH_D, 3 * HP), jnp.float32) * s, 'dense_wo': jax.random.normal(ks[5], (NH_D * HP, H), jnp.float32) * s}
    _L0_ffn_in = _L0_ffn_setup()
    _d = {'L0_attn_x': _L0_attn_in['x'], 'L0_attn_Wq': _L0_attn_in['Wq'], 'L0_attn_bq': _L0_attn_in['bq'], 'L0_attn_Wk': _L0_attn_in['Wk'], 'L0_attn_bk': _L0_attn_in['bk'], 'L0_attn_Wv': _L0_attn_in['Wv'], 'L0_attn_bv': _L0_attn_in['bv'], 'L0_attn_Wo': _L0_attn_in['Wo'], 'L0_attn_bo': _L0_attn_in['bo'], 'L0_ffn_mosa_router_w': _L0_ffn_in['mosa_router_w'], 'L0_ffn_mosa_wqkv': _L0_ffn_in['mosa_wqkv'], 'L0_ffn_mosa_wo': _L0_ffn_in['mosa_wo'], 'L0_ffn_dense_wqkv': _L0_ffn_in['dense_wqkv'], 'L0_ffn_dense_wo': _L0_ffn_in['dense_wo']}
    _x0 = _d['L0_attn_x']
    _d['L0_attn_x'] = jax.random.normal(jax.random.fold_in(jax.random.key(seed), 1), (4, 2048, 256), dtype=_x0.dtype)
    del _x0
    return _d

def reference(L0_attn_x, L0_attn_Wq, L0_attn_bq, L0_attn_Wk, L0_attn_bk, L0_attn_Wv, L0_attn_bv, L0_attn_Wo, L0_attn_bo, L0_ffn_mosa_router_w, L0_ffn_mosa_wqkv, L0_ffn_mosa_wo, L0_ffn_dense_wqkv, L0_ffn_dense_wo):

    def _L0_attn_ref(x, Wq, bq, Wk, bk, Wv, bv, Wo, bo):
        import jax, jax.numpy as jnp
        import numpy as np
        EMBED = 256
        HEADS = 16
        HEAD_DIM = EMBED // HEADS
        B, T = (2, 512)
        ROPE_THETA = 10000.0

        def _rope(x):
            D = x.shape[-1]
            inv_freq = 1.0 / ROPE_THETA ** (jnp.arange(0, D, 2, dtype=jnp.float32) / D)
            freqs = jnp.arange(x.shape[2], dtype=jnp.float32)[:, None] * inv_freq[None, :]
            cos = jnp.cos(freqs).astype(x.dtype)
            sin = jnp.sin(freqs).astype(x.dtype)
            x1, x2 = (x[..., :D // 2], x[..., D // 2:])
            return jnp.concatenate([x1 * cos - x2 * sin, x2 * cos + x1 * sin], axis=-1)
        Bb, Tt, C = x.shape
        H, D = (HEADS, HEAD_DIM)

        def proj(W, b):
            return (jnp.einsum('btc,oc->bto', x, W) + b).reshape(Bb, Tt, H, D).transpose(0, 2, 1, 3)
        q = _rope(proj(Wq, bq))
        k = _rope(proj(Wk, bk))
        v = proj(Wv, bv)
        scale = jnp.sqrt(jnp.asarray(D, dtype=x.dtype))
        scores = jnp.einsum('bhtd,bhsd->bhts', q, k) / scale
        attn = jax.nn.softmax(scores, axis=-1)
        out = jnp.einsum('bhts,bhsd->bhtd', attn, v)
        out = out.transpose(0, 2, 1, 3).reshape(Bb, Tt, C)
        return jnp.einsum('btc,oc->bto', out, Wo) + bo

    def _L0_ffn_ref(X, mosa_router_w, mosa_wqkv, mosa_wo, dense_wqkv, dense_wo):
        import jax, jax.numpy as jnp
        import numpy as np
        H, HP, NH_M, NH_D = (256, 64, 8, 8)
        B, T = (2, 512)
        SPARSITY = 8
        N_ROT = 32
        BASE = 10000.0

        def _rope(x, pos, n_rot, base):
            half = n_rot // 2
            inv = base ** (-jnp.arange(half, dtype=x.dtype) / half)
            ang = pos[..., None] * inv
            cos, sin = (jnp.cos(ang), jnp.sin(ang))
            x1, x2 = (x[..., :half], x[..., half:n_rot])
            rot = jnp.concatenate([x1 * cos - x2 * sin, x1 * sin + x2 * cos], axis=-1)
            return jnp.concatenate([rot, x[..., n_rot:]], axis=-1)

        def _mosa_branch(X, router_w, wqkv, wo):
            b, t, _ = X.shape
            k = t // SPARSITY
            scores = jnp.einsum('bth,hn->bnt', X, router_w)
            _, idx = jax.lax.top_k(scores, k)
            idx = jnp.sort(idx, axis=-1)
            gates = jax.nn.sigmoid(jnp.take_along_axis(scores, idx, axis=-1))
            Xg = jnp.take_along_axis(X[:, None], idx[..., None], axis=2)
            qkv = jnp.einsum('bnkh,hnd->bnkd', Xg, wqkv)
            Q, K, V = jnp.split(qkv, 3, axis=-1)
            pos = idx.astype(X.dtype)
            Q = _rope(Q, pos, N_ROT, BASE)
            K = _rope(K, pos, N_ROT, BASE)
            att = jnp.einsum('bnqd,bnkd->bnqk', Q, K) / jnp.sqrt(jnp.asarray(HP, X.dtype))
            causal = idx[..., :, None] >= idx[..., None, :]
            att = jnp.where(causal, att, -jnp.inf)
            AV = jnp.einsum('bnqk,bnkd->bnqd', jax.nn.softmax(att, axis=-1), V)
            AV = AV * gates[..., None]
            out = jnp.zeros((b, NH_M, t, HP), X.dtype)
            bi = jnp.arange(b)[:, None, None]
            hi = jnp.arange(NH_M)[None, :, None]
            out = out.at[bi, hi, idx].set(AV)
            out = out.transpose(0, 2, 1, 3).reshape(b, t, NH_M * HP)
            return out @ wo

        def _dense_branch(X, wqkv, wo):
            b, t, _ = X.shape
            qkv = jnp.einsum('bth,hnd->bntd', X, wqkv)
            Q, K, V = jnp.split(qkv, 3, axis=-1)
            pos = jnp.arange(t, dtype=X.dtype)
            Q = _rope(Q, pos, N_ROT, BASE)
            K = _rope(K, pos, N_ROT, BASE)
            att = jnp.einsum('bnqd,bnkd->bnqk', Q, K) / jnp.sqrt(jnp.asarray(HP, X.dtype))
            causal = jnp.tril(jnp.ones((t, t), bool))
            att = jnp.where(causal, att, -jnp.inf)
            AV = jnp.einsum('bnqk,bnkd->bnqd', jax.nn.softmax(att, axis=-1), V)
            return AV.transpose(0, 2, 1, 3).reshape(b, t, NH_D * HP) @ wo
        return _mosa_branch(X, mosa_router_w, mosa_wqkv, mosa_wo) + _dense_branch(X, dense_wqkv, dense_wo)
    x = L0_attn_x
    x = _layernorm(x + _L0_attn_ref(x, L0_attn_Wq, L0_attn_bq, L0_attn_Wk, L0_attn_bk, L0_attn_Wv, L0_attn_bv, L0_attn_Wo, L0_attn_bo), axis=-1)
    x = _layernorm(x + _L0_ffn_ref(x, L0_ffn_mosa_router_w, L0_ffn_mosa_wqkv, L0_ffn_mosa_wo, L0_ffn_dense_wqkv, L0_ffn_dense_wo), axis=-1)
    return x

_drawn_inputs = setup_inputs


def setup_inputs(seed=0):
    import zlib

    import numpy as np

    out = dict(_drawn_inputs(seed))
    spreads = {'L0_attn_bq': (0.0, 0.8),
     'L0_attn_bk': (0.0, 0.8),
     'L0_attn_bv': (0.0, 0.1),
     'L0_attn_bo': (0.0, 0.1)}
    factors = {'L0_ffn_mosa_router_w': 7.963,
     'L0_ffn_mosa_wqkv': 7.831,
     'L0_ffn_mosa_wo': 7.535,
     'L0_ffn_dense_wqkv': 2.705,
     'L0_ffn_dense_wo': 2.752}
    for name, (base, spread) in spreads.items():
        noise = np.random.default_rng([zlib.crc32(name.encode()), seed]).standard_normal(out[name].shape)
        drawn = base * np.exp(spread * noise) if base else spread * noise
        out[name] = jnp.asarray(drawn.astype(out[name].dtype))
    for name, factor in factors.items():
        out[name] = (out[name] * factor).astype(out[name].dtype)
    return out
```

```python
import concourse.bass as bass
from concourse import mybir
from contextlib import ExitStack

FP32 = mybir.dt.float32
BF16 = mybir.dt.bfloat16
U32 = mybir.dt.uint32
ALU = mybir.AluOpType
ACT = mybir.ActivationFunctionType
AX = mybir.AxisListType

P = 128
B, T, C = 4, 2048, 256
HEADS, HD = 16, 16
CT = C // P
TT = T // P
CH = 512
NCH = T // CH
NBH = B * HEADS
VW = 32
PARTS = 3
STACK = 6 * HD
MROWS = 3
HALF = T // 2


def scope(nc, ctx):
    def sb(name, shape, dt):
        return ctx.enter_context(nc.sbuf_tensor(name, shape, dt))

    def pb(name, shape, dt=FP32):
        return ctx.enter_context(nc.psum_tensor(name, shape, dt))

    def sem(name):
        return ctx.enter_context(nc.semaphore(name))
    return sb, pb, sem


def project_attention(nc, d):
    ctx = ExitStack()
    with ctx:
        sb, pb, sem = scope(nc, ctx)
        XT = [sb(f"a_xT{i}", [P, CT, T], FP32) for i in range(2)]
        W = sb("a_w", [P, CT, 5, C], FP32)
        BIAS = sb("a_bias", [P, 4, CT], FP32)
        BV = sb("a_bv", [1, C], FP32)
        ONES = sb("a_ones", [1, P], FP32)
        COS = sb("a_cos", [P, T], FP32)
        SIN = sb("a_sin", [P, T], FP32)
        T1 = sb("a_t1", [P, 2, CH], FP32)
        T2 = sb("a_t2", [P, 2, CH], FP32)
        F = sb("a_f", [P, 2, CH], FP32)
        R = sb("a_r", [P, 2, CH], FP32)
        S = [sb(f"a_s{i}", [P, PARTS, T], BF16) for i in range(2)]
        V = sb("a_v", [P, HEADS, TT, VW], FP32)
        PA = [pb(f"a_pa{i}", [P, CH]) for i in range(2)]
        PB = [pb(f"a_pb{i}", [P, CH]) for i in range(2)]
        PV = [pb(f"a_pv{i}", [P, CH]) for i in range(2)]
        const_in = sem("a_const_in")
        x_in = [sem(f"a_x_in{i}") for i in range(2)]
        v_init = sem("a_v_init")
        xt_free = sem("a_xt_free")
        qk_ready = sem("a_qk_ready")
        qk_read = sem("a_qk_read")
        rope_link = sem("a_rope_link")
        f_ready = sem("a_f_ready")
        hi_ready = sem("a_hi_ready")
        r_ready = sem("a_r_ready")
        mid_ready = sem("a_mid_ready")
        lo_ready = sem("a_lo_ready")
        s_out = [sem(f"a_s_out{i}") for i in range(2)]
        v_ready = sem("a_v_ready")
        v_copied = sem("a_v_copied")
        v_out = sem("a_v_out")
        G = 2 * CT * NCH
        block = ctx.enter_context(nc.Block())

        @block.sync
        def _(sp):
            sp.dma_start(W[:, :, :, :], d["wqkv"].rearrange("(c p) w o -> p c w o", p=P)).then_inc(const_in, 16)
            sp.dma_start(BIAS[:, :, :], d["bqk"]).then_inc(const_in, 16)
            sp.dma_start(BV[:, :], d["bv"]).then_inc(const_in, 16)
            sp.dma_start(COS[:, :], d["cos16"]).then_inc(const_in, 16)
            sp.dma_start(SIN[:, :], d["sin16"]).then_inc(const_in, 16)
            with sp.Fori(0, B // 2) as bb:
                for i in range(2):
                    sp.wait_ge(xt_free, bb * 2 + 1)
                    sp.dma_start(XT[i][:, :, :], d["xT"][bass.ds(bb * 2 + i, 1)].rearrange("b (c p) t -> p (b c) t", p=P)).then_inc(x_in[i], 16)
                for i in range(2):
                    b = bb * 2 + i
                    for tile in range(2 * CT):
                        qk, ot = tile // CT, tile % CT
                        sp.wait_ge(lo_ready, b * G + (tile + 1) * NCH)
                        sp.dma_start(d["qs" if qk == 0 else "ks"][:, bass.ds(b * C + ot * P, P), :]
                                     .rearrange("s p t -> p s t"), S[tile % 2][:, :, :]).then_inc(s_out[tile % 2], 16)
                    sp.wait_ge(v_copied, (b + 1) * TT)
                    sp.dma_start(d["vs"][bass.ds(b * HEADS, HEADS), :, :].rearrange("h p f -> p h f"),
                                 V[:, :, :, :].rearrange("p h t f -> p h (t f)")).then_inc(v_out, 16)
            for i in range(2):
                sp.wait_ge(s_out[i], 16 * CT * B)
            sp.wait_ge(v_out, 16 * B)

        @block.gpsimd
        def _(pool):
            nc.gpsimd.memset(V[:, :, :, :], 0.0).then_inc(v_init, 1)
            pool.wait_ge(v_init, 1)
            nc.gpsimd.memset(V[:, :, :, HD:HD + 1], 1.0).then_inc(v_init, 1)
            nc.gpsimd.memset(ONES[:, :], 1.0).then_inc(v_init, 1)
            pool.sem_inc(xt_free, 1)
            with pool.Fori(0, B // 2) as bb:
                for i in range(2):
                    b = bb * 2 + i
                    for g in range(G):
                        tile, ch = g // NCH, g % NCH
                        pool.wait_ge(hi_ready, b * G + g + 1)
                        if g >= 2 or i >= 1:
                            pool.wait_ge(lo_ready, b * G + g - 1)
                        nc.gpsimd.tensor_tensor(R[:, g % 2, :], F[:, g % 2, :],
                                                S[tile % 2][:, 0, ch * CH:(ch + 1) * CH], ALU.subtract).then_inc(r_ready, 1)
                pool.wait_ge(lo_ready, bb * (2 * G) + 2 * G)
                pool.wait_ge(v_ready, bb * (2 * TT) + 2 * TT)
                pool.sem_inc(xt_free, 2)

        @block.tensor
        def _(pe):
            pe.wait_ge(const_in, 16 * 5)
            pe.wait_ge(v_init, 3)
            with pe.Fori(0, B // 2) as bb:
                for i in range(2):
                    b = bb * 2 + i
                    pe.wait_ge(x_in[i], bb * 16 + 16)
                    for g in range(G):
                        qk, ot, ch = g // (CT * NCH), (g // NCH) % CT, g % NCH
                        if g >= 2 or i >= 1:
                            pe.wait_ge(qk_read, b * G + g - 1)
                        for w, dst in ((2 * qk, PA), (2 * qk + 1, PB)):
                            for c in range(CT):
                                last = pe.matmul(dst[g % 2][:, :], W[:, c, w, ot * P:(ot + 1) * P],
                                                 XT[i][:, c, ch * CH:(ch + 1) * CH], start=(c == 0), stop=(c == CT - 1))
                        last.then_inc(qk_ready, 1)
                    for t in range(TT):
                        if t >= 2 or i >= 1:
                            pe.wait_ge(v_copied, b * TT + t - 1)
                        for c in range(CT):
                            pe.matmul(PV[t % 2][:, 0:C], XT[i][:, c, t * P:(t + 1) * P], W[:, c, 4, :],
                                      start=(c == 0), stop=False)
                        pe.matmul(PV[t % 2][:, 0:C], ONES[:, :], BV[:, :], start=False, stop=True).then_inc(v_ready, 1)
                if B > 2:
                    pe.wait_ge(qk_read, bb * (2 * G) + 2 * G)
                    pe.wait_ge(v_copied, bb * (2 * TT) + 2 * TT)

        @block.vector
        def _(dve):
            dve.wait_ge(const_in, 16 * 5)
            dve.wait_ge(v_init, 3)
            with dve.Fori(0, B // 2) as bb:
                for i in range(2):
                    b = bb * 2 + i

                    def low_part(g):
                        dve.wait_ge(mid_ready, b * G + g + 1)
                        tile, ch = g // NCH, g % NCH
                        nc.vector.tensor_tensor(S[tile % 2][:, 2, ch * CH:(ch + 1) * CH], R[:, g % 2, :],
                                                S[tile % 2][:, 1, ch * CH:(ch + 1) * CH], ALU.subtract).then_inc(lo_ready, 1)

                    for g in range(G):
                        qk, ot, ch = g // (CT * NCH), (g // NCH) % CT, g % NCH
                        dve.wait_ge(qk_ready, b * G + g + 1)
                        nc.vector.scalar_tensor_tensor(T1[:, g % 2, :], PA[g % 2][:, :], BIAS[:, 2 * qk, ot:ot + 1],
                                                       COS[:, ch * CH:(ch + 1) * CH], ALU.add, ALU.mult)
                        nc.vector.scalar_tensor_tensor(T2[:, g % 2, :], PB[g % 2][:, :], BIAS[:, 2 * qk + 1, ot:ot + 1],
                                                       SIN[:, ch * CH:(ch + 1) * CH], ALU.add, ALU.mult).then_inc(qk_read, 1)
                        dve.wait_ge(qk_read, b * G + g + 1)
                        nc.vector.tensor_tensor(F[:, g % 2, :], T1[:, g % 2, :], T2[:, g % 2, :], ALU.add).then_inc(f_ready, 1)
                        if g >= 1:
                            low_part(g - 1)
                    low_part(G - 1)

        @block.scalar
        def _(act):
            act.wait_ge(v_init, 3)
            with act.Fori(0, B // 2) as bb:
                for i in range(2):
                    b = bb * 2 + i
                    def middle_part(g):
                        tile, ch = g // NCH, g % NCH
                        act.wait_ge(r_ready, b * G + g + 1)
                        nc.scalar.copy(S[tile % 2][:, 1, ch * CH:(ch + 1) * CH], R[:, g % 2, :]).then_inc(mid_ready, 1)

                    for g in range(G):
                        tile, ch = g // NCH, g % NCH
                        if ch == 0:
                            if tile >= 2:
                                act.wait_ge(s_out[tile % 2], (b * CT + tile // 2) * 16)
                            elif i == 1:
                                act.wait_ge(s_out[tile % 2], b * CT * 16)
                        act.wait_ge(f_ready, b * G + g + 1)
                        nc.scalar.copy(S[tile % 2][:, 0, ch * CH:(ch + 1) * CH], F[:, g % 2, :]).then_inc(hi_ready, 1)
                        if g >= 1:
                            middle_part(g - 1)
                    middle_part(G - 1)
                    if i == 1:
                        act.wait_ge(v_out, b * 16)
                    for t in range(TT):
                        act.wait_ge(v_ready, b * TT + t + 1)
                        nc.scalar.copy(V[:, :, t, 0:HD], PV[t % 2][:, 0:C].rearrange("p (h f) -> p h f", h=HEADS)).then_inc(v_copied, 1)
                act.wait_ge(v_out, bb * 32 + 32)
                for s in range(2):
                    act.wait_ge(s_out[s], (bb * 2 + 2) * CT * 16)


NB = 4
UNITS = NCH * TT // 2
NCK = TT * NCH
LEAD = 4
PSLOTS = 4
MSLOTS = 3
OUTW = TT // 2 * 32


def full_attention(nc, d):
    ctx = ExitStack()
    with ctx:
        sb, pb, sem = scope(nc, ctx)
        ATT = d["ATT"]
        Q = [sb(f"b_q{i}", [P, T], BF16) for i in range(NB)]
        K = [sb(f"b_k{i}", [P, T], BF16) for i in range(NB)]
        V = [sb(f"b_v{i}", [P, TT, VW], FP32) for i in range(NB)]
        E = sb("b_e", [P, PSLOTS, HALF], FP32)
        MX = sb("b_mx", [P, TT, NCH], FP32)
        NEG = sb("b_neg", [P, 3, TT], FP32)
        NP = sb("b_np", [P, P // TT, TT], BF16)
        MT = sb("b_mt", [PARTS * TT, P], BF16)
        OT = sb("b_ot", [P, T], FP32)
        DEN = sb("b_den", [P, 2, TT // 2, 1], FP32)
        SEL = sb("b_sel", [P, HD + 1], FP32)
        IDB = sb("b_idb", [P, P], BF16)
        PS = [pb(f"b_ps{i}", [P, HALF]) for i in range(2)]
        PO = pb("b_po", [P, CH])
        PM = [pb(f"b_pm{i}", [P, CH]) for i in range(MSLOTS)]
        const_in = sem("b_const_in")
        init = sem("b_init")
        head_in = [sem(f"b_head_in{i}") for i in range(NB)]
        s_ready = sem("b_s_ready")
        e_ready = sem("b_e_ready")
        ring_ready = sem("b_ring_ready")
        ring_read = sem("b_ring_read")
        av_quad = sem("b_av_quad")
        ot_ready = sem("b_ot_ready")
        neg_ready = sem("b_neg_ready")
        m_in = sem("b_m_in")
        link = sem("b_link")
        den_ready = sem("b_den_ready")
        RING = NCK + 2

        def plan():
            uses = []
            for u in range(UNITS):
                now = []
                if u == LEAD + 1:
                    now.append(("out", -1, 1))
                for k in range(2):
                    c = 2 * (u + LEAD) + k
                    now.append(("chunk", 1 + c // NCK, c % NCK))
                if u == UNITS - LEAD:
                    now.append(("turn", 1, 1))
                uses.append(now)
            return uses
        PLAN = plan()

        def steps(first, last, e, peeled):
            for u in range(UNITS):
                yield ("scores", u)
                for place, (kind, dh, k) in enumerate(PLAN[u]):
                    if place == len(PLAN[u]) // 2 and u % 2 == 1 and not (first and e == 0 and u < 2):
                        yield ("values", u // 2 - 1)
                    if peeled and dh > 0 and e + dh >= NB:
                        continue
                    if first and e + dh < 0:
                        continue
                    yield (kind, e + dh, k)
            if last and e == NB - 1:
                yield ("values", UNITS // 2 - 1)
                yield ("out", e, 0)
                yield ("out", e, 1)

        block = ctx.enter_context(nc.Block())
        ITERS = NBH // NB

        def schedule(part):
            out = []
            if part == "first":
                out += [("load", h, 0) for h in range(3)]
                out += [("chunk", 0, c) for c in range(NCK)] + [("turn", 0, 0)]
                out += [("chunk", 1, c) for c in range(2 * LEAD)]
            for e in range(NB):
                if not (part == "last" and e > 0):
                    out.append(("load", e + 3, 0))
                out += [(s[0], e, s[1]) if s[0] in ("scores", "values") else s
                        for s in steps(part == "first", part == "last", e, part == "last")]
            return out
        FIRST, MIDDLE, LAST = schedule("first"), schedule("middle"), schedule("last")

        def count(sched, kinds):
            return sum(1 for s in sched if s[0] in kinds)
        RINGK = ("chunk", "turn", "out")
        assert count(MIDDLE, RINGK) == NB * RING and NB * RING % MSLOTS == 0
        R0 = count(FIRST, RINGK)

        def run(engine, step):
            def pass_over(sched, i, base):
                n = dict(ring=0, scores=0, values=0, par=0)
                n.update(base)
                for s in sched:
                    step(s, i, n)
                    n["par"] = (n["par"] + (s[0] in RINGK)) % MSLOTS
                    key = "ring" if s[0] in RINGK else s[0]
                    n[key] = n.get(key, 0) + 1
                return n
            n0 = pass_over(FIRST, 0, {})
            with engine.Fori(1, ITERS - 1) as i:
                grow = dict(ring=NB * RING, scores=NB * UNITS, values=NB * UNITS // 2)
                base = {k: (i - 1) * g + n0.get(k, 0) for k, g in grow.items()}
                base["par"] = R0 % MSLOTS
                n = pass_over(MIDDLE, i, base)
            last = {k: (ITERS - 2) * g + n0.get(k, 0) for k, g in grow.items()}
            last["par"] = R0 % MSLOTS
            pass_over(LAST, ITERS - 1, last)

        @block.sync
        def _(sp):
            sp.dma_start(SEL[:, :], d["sel17"]).then_inc(const_in, 16)
            sp.dma_start(IDB[:, :], d["ident_bf16"]).then_inc(const_in, 16)

            def step(s, i, n):
                kind, e, k = s
                h = i * NB + e
                if kind == "load":
                    slot = e % NB
                    if not (isinstance(i, int) and i == 0 and e < NB):
                        sp.wait_ge(av_quad, (h - NB + 1) * (UNITS // 2))
                    rows = bass.ds(h * HD, HD)
                    dma = [(Q[slot][0:3 * HD, :], d["qs"][0:3, rows, :]),
                           (Q[slot][3 * HD:5 * HD, :], d["qs"][0:2, rows, :]),
                           (Q[slot][5 * HD:6 * HD, :], d["qs"][0:1, rows, :])]
                    for r, part in enumerate((0, 0, 0, 1, 1, 2)):
                        dma.append((K[slot][r * HD:(r + 1) * HD, :], d["ks"][part:part + 1, rows, :]))
                    for dst, src in dma:
                        sp.dma_start(dst, src).then_inc(head_in[slot], 16)
                    sp.dma_start(V[slot][:, :, :], d["vs"][bass.ds(h, 1), :, :].rearrange("h p (t f) -> p (h t) f", f=VW)).then_inc(head_in[slot], 16)
                elif kind == "turn":
                    sp.wait_ge(ring_read, n["ring"] + 1)
                    for r in range(PARTS):
                        sp.dma_start(Q[e % NB][STACK + r:STACK + r + 1, :], MT[r * TT:(r + 1) * TT, :]).then_inc(m_in, 16)
            run(sp, step)
            sp.wait_ge(m_in, 16 * 3 * NBH)

        LOADS = 10 * 16

        @block.gpsimd
        def _(pool):
            for i in range(NB):
                nc.gpsimd.memset(K[i][STACK:P, :], 1.0).then_inc(init, 1)
            pool.wait_ge(init, NB)
            nc.gpsimd.memset(NP[:, :, :], 0.0).then_inc(init, 1)

        @block.tensor
        def _(pe):
            pe.wait_ge(const_in, 32)
            pe.wait_ge(init, NB + 1)

            def ring_slot(n):
                if not (isinstance(n["ring"], int) and n["ring"] < MSLOTS):
                    pe.wait_ge(ring_read, n["ring"] - MSLOTS + 1)
                return PM[n["par"]]

            def step(s, i, n):
                kind, e, k = s
                h = i * NB + e
                if kind == "scores":
                    quarter, pair = k // (TT // 2), k % (TT // 2)
                    if k == 0:
                        pe.wait_ge(m_in, (h + 1) * 16 * 3)
                    if not (isinstance(i, int) and i == 0 and e == 0 and k < 2):
                        pe.wait_ge(e_ready, n["scores"] - 1)
                    for c in range(2):
                        j = 2 * pair + c
                        last = pe.matmul(PS[k % 2][:, c * CH:(c + 1) * CH], K[e % NB][0:STACK + MROWS, j * P:(j + 1) * P],
                                         Q[e % NB][0:STACK + MROWS, quarter * CH:(quarter + 1) * CH], start=True, stop=True)
                    last.then_inc(s_ready, 1)
                elif kind == "chunk":
                    t, c = k // NCH, k % NCH
                    if k == 0:
                        pe.wait_ge(head_in[e % NB], (i + e // NB + 1) * LOADS)
                    pm = ring_slot(n)
                    pe.matmul(pm[:, :], Q[e % NB][0:STACK, t * P:(t + 1) * P], K[e % NB][0:STACK, c * CH:(c + 1) * CH],
                              start=True, stop=True).then_inc(ring_ready, 1)
                elif kind == "turn":
                    pe.wait_ge(neg_ready, h + 1)
                    pm = ring_slot(n)
                    last = pe.transpose(pm[:, OUTW:OUTW + P // 2].bitcast(BF16),
                                        NP[:, :, :].rearrange("p a t -> p (a t)"), IDB[:, :])
                    if k:
                        last = output(pm, h - 1, 0)
                    last.then_inc(ring_ready, 1)
                elif kind == "values":
                    quarter, quad = k // (TT // 4) % NCH, k % (TT // 4)
                    hv = e if k >= 0 else e - 1
                    pe.wait_ge(e_ready, n["values"] * 2 + 2)
                    if quad == 0 and not (isinstance(i, int) and i == 0 and e == 0 and quarter == 0):
                        pe.wait_ge(ot_ready, (i * NB + hv) * NCH + quarter)
                    for g in range(4):
                        last = pe.matmul(PO[g * VW:(g + 1) * VW, :], V[hv % NB][:, quad * 4 + g, :],
                                         E[:, (2 * k + g // 2) % PSLOTS, g % 2 * CH:(g % 2 + 1) * CH],
                                         start=(quad == 0), stop=(quad == TT // 4 - 1))
                    last.then_inc(av_quad, 1)
                elif kind == "out":
                    pm = ring_slot(n)
                    output(pm, h, k).then_inc(ring_ready, 1)

            def output(pm, h, half):
                pe.wait_ge(ot_ready, (h * 2 + half + 1) * 2)
                for t in range(TT // 2):
                    last = pe.matmul(pm[:, t * 32:t * 32 + HD + 1], OT[:, half * HALF + t * P:half * HALF + (t + 1) * P], SEL[:, :],
                                     start=True, stop=True)
                return last
            run(pe, step)

        @block.scalar
        def _(act):
            def step(s, i, n):
                kind, e, k = s
                if kind == "scores":
                    act.wait_ge(s_ready, n["scores"] + 1)
                    if not (isinstance(i, int) and i == 0 and e == 0 and k < PSLOTS) and k % 2 == 0:
                        act.wait_ge(av_quad, (i * NB + e) * (UNITS // 2) + k // 2 - PSLOTS // 2 + 1)
                    nc.scalar.activation(E[:, k % PSLOTS, :], PS[k % 2][:, :], ACT.Exp, scale=HD ** -0.5).then_inc(e_ready, 1)
            run(act, step)

        @block.vector
        def _(dve):
            dve.wait_ge(init, NB + 1)

            def step(s, i, n):
                kind, e, k = s
                h = i * NB + e
                if kind == "values" and k % (TT // 4) == TT // 4 - 1:
                    quarter = k // (TT // 4) % NCH
                    dve.wait_ge(av_quad, n["values"] + 1)
                    nc.vector.tensor_copy(OT[:, quarter * CH:(quarter + 1) * CH], PO[:, :]).then_inc(ot_ready, 1)
                if kind in RINGK:
                    dve.wait_ge(ring_ready, n["ring"] + 1)
                    pm = PM[n["par"]]
                if kind == "chunk":
                    t, c = k // NCH, k % NCH
                    nc.vector.reduce_max(MX[:, t, c:c + 1], pm[:, :], AX.X).then_inc(ring_read, 1)
                    if k == NCK - 1:
                        dve.wait_ge(ring_read, n["ring"] + 1)
                        nc.vector.tensor_reduce(NEG[:, 0, :], MX[:, :, :], AX.X, ALU.max, negate=True).then_inc(link, 1)
                        dve.wait_ge(link, h * 4 + 1)
                        nc.vector.tensor_copy(NP[:, 0, :], NEG[:, 0, :]).then_inc(link, 1)
                        dve.wait_ge(link, h * 4 + 2)
                        nc.vector.tensor_tensor(NEG[:, 1, :], NEG[:, 0, :], NP[:, 0, :], ALU.subtract).then_inc(link, 1)
                        dve.wait_ge(link, h * 4 + 3)
                        nc.vector.tensor_copy(NP[:, 1, :], NEG[:, 1, :]).then_inc(link, 1)
                        dve.wait_ge(link, h * 4 + 4)
                        nc.vector.tensor_tensor(NP[:, 2, :], NEG[:, 1, :], NP[:, 1, :], ALU.subtract).then_inc(neg_ready, 1)
                elif kind == "turn":
                    if not (isinstance(i, int) and i == 0 and e == 0):
                        dve.wait_ge(m_in, h * 16 * 3)
                    last = nc.vector.tensor_copy(MT[:, :], pm[:, OUTW:OUTW + P // 2].bitcast(BF16)[0:PARTS * TT, :])
                    if k:
                        last = output(pm, h - 1, 0)
                    last.then_inc(ring_read, 1)
                elif kind == "out":
                    output(pm, h, k).then_inc(ring_read, 1)

            def output(pm, h, half):
                o = pm[:, 0:OUTW].rearrange("p (t f) -> p t f", f=32)
                nc.vector.reciprocal(DEN[:, half, :, :], o[:, :, HD:HD + 1]).then_inc(den_ready, 1)
                dve.wait_ge(den_ready, h * 2 + half + 1)
                return nc.vector.tensor_tensor(ATT[:, bass.ds(h * TT + half * (TT // 2), TT // 2), :], o[:, :, 0:HD],
                                               DEN[:, half, :, :].to_broadcast([P, TT // 2, HD]), ALU.mult)
            run(dve, step)


EPS = 1e-5
DH = 8
DD = 64
ROT = 32
TOP = T // 8
NEGBIG = -1e30


def first_norm(nc, d):
    ctx = ExitStack()
    with ctx:
        sb, pb, sem = scope(nc, ctx)
        ATT = d["ATT"][:, :, :].rearrange("p (n t) f -> p n t f", t=TT)
        X1T = d["X1T"]
        WO = sb("c_wo", [P, CT, C], FP32)
        BO = sb("c_bo", [1, C], FP32)
        ONES = sb("c_ones", [1, P], FP32)
        IDF = sb("c_idf", [P, P], FP32)
        WV = sb("c_wv", [P, CT, DH * DD], FP32)
        XB = sb("c_x", [P, TT, C], FP32)
        STG = [sb(f"c_stg{i}", [P, C], FP32) for i in range(2)]
        AT = [sb(f"c_at{i}", [P, CT, P], FP32) for i in range(2)]
        ST = sb("c_st", [P, TT, 6], FP32)
        MV = sb("c_mv", [P, TT, 2], FP32)
        STD = sb("c_std", [P, TT], FP32)
        MARK = sb("c_mark", [P, 1], FP32)
        RSTD = sb("c_rstd", [P, TT], FP32)
        VD = [sb(f"c_vd{i}", [P, DH * DD], FP32) for i in range(2)]
        PT = [pb(f"c_pt{i}", [P, CT, P]) for i in range(2)]
        PY = [pb(f"c_py{i}", [P, C]) for i in range(2)]
        PV = [pb(f"c_pv{i}", [P, DH * DD]) for i in range(2)]
        const_in = sem("c_const_in")
        ones_set = sem("c_ones_set")
        x_in = sem("c_x_in")
        staged = sem("c_staged")
        turned = sem("c_turned")
        copied = sem("c_copied")
        y_ready = sem("c_y_ready")
        sum_ready = sem("c_sum_ready")
        stat_ready = sem("c_stat_ready")
        aggr_ready = sem("c_aggr_ready")
        var_ready = sem("c_var_ready")
        std_ready = sem("c_std_ready")
        rstd_ready = sem("c_rstd_ready")
        norm_ready = sem("c_norm_ready")
        x1t_ready = sem("c_x1t_ready")
        vd_ready = sem("c_vd_ready")
        vd_copied = sem("c_vd_copied")
        vd_out = [sem(f"c_vd_out{i}") for i in range(2)]
        x1_out = sem("c_x1_out")
        block = ctx.enter_context(nc.Block())

        @block.sync
        def _(sp):
            sp.dma_start(WO[:, :, :], d["woT"].rearrange("(c p) o -> p c o", p=P)).then_inc(const_in, 16)
            sp.dma_start(BO[:, :], d["bo"]).then_inc(const_in, 16)
            sp.dma_start(IDF[:, :], d["ident"]).then_inc(const_in, 16)
            sp.dma_start(WV[:, :, :], d["wdv"].rearrange("(c p) o -> p c o", p=P)).then_inc(const_in, 16)

            def load_x(b):
                sp.dma_start(XB[:, :, :], d["x"][bass.ds(b, 1), :, :].rearrange("b (t p) c -> p (b t) c", p=P)).then_inc(x_in, 16)

            def stores(b):
                for t in range(TT):
                    sp.wait_ge(vd_copied, b * TT + t + 1)
                    sp.dma_start(d["vd"][bass.ds(b * DH, DH), :, t, :].rearrange("n p f -> p n f"),
                                 VD[t % 2][:, :].rearrange("p (n f) -> p n f", n=DH)).then_inc(vd_out[t % 2], 16)
                sp.wait_ge(norm_ready, b * TT + TT)
                for name in ("x1", "y"):
                    sp.dma_start(d[name][bass.ds(b * T, T), :].rearrange("(t p) c -> p t c", p=P), XB[:, :, :]).then_inc(x1_out, 16)
            load_x(0)
            with sp.Fori(0, B - 1) as b:
                stores(b)
                sp.wait_ge(x1_out, b * 32 + 32)
                load_x(b + 1)
            stores(B - 1)
            sp.wait_ge(x1_out, B * 32)
            for i in range(2):
                sp.wait_ge(vd_out[i], 16 * B * TT // 2)

        @block.gpsimd
        def _(pool):
            nc.gpsimd.memset(ONES[:, :], 1.0).then_inc(ones_set, 1)
            with pool.Fori(0, B) as b:
                for t in range(TT):
                    if t >= 2:
                        pool.wait_ge(turned, b * 2 * TT + t - 1)
                    nc.gpsimd.tensor_copy(STG[t % 2][:, :].rearrange("p (n f) -> p n f", f=HD),
                                          ATT[:, bass.ds(b * HEADS, HEADS), t, :]).then_inc(staged, 1)
                for t in range(TT):
                    pool.wait_ge(copied, b * 2 * TT + TT + t + 1)
                    nc.gpsimd.tensor_copy(X1T[:, :, bass.ds(b * T + t * P, P)], AT[t % 2][:, :, :]).then_inc(x1t_ready, 1)

        @block.tensor
        def _(pe):
            pe.wait_ge(const_in, 64)
            pe.wait_ge(ones_set, 1)
            with pe.Fori(0, B) as b:
                def project(t):
                    pe.wait_ge(copied, b * 2 * TT + t + 1)
                    if t >= 2:
                        pe.wait_ge(sum_ready, b * TT + t - 1)
                    for c in range(CT):
                        pe.matmul(PY[t % 2][:, :], AT[t % 2][:, c, :], WO[:, c, :], start=(c == 0), stop=False)
                    pe.matmul(PY[t % 2][:, :], ONES[:, :], BO[:, :], start=False, stop=True).then_inc(y_ready, 1)
                for t in range(TT):
                    pe.wait_ge(staged, b * TT + t + 1)
                    if t >= 2:
                        pe.wait_ge(copied, b * 2 * TT + t - 1)
                    for c in range(CT):
                        last = pe.transpose(PT[t % 2][:, c, :], STG[t % 2][:, c * P:(c + 1) * P], IDF[:, :])
                    last.then_inc(turned, 1)
                    if t >= 1:
                        project(t - 1)
                project(TT - 1)

                def values(t):
                    pe.wait_ge(copied, b * 2 * TT + TT + t + 1)
                    if t >= 2:
                        pe.wait_ge(vd_copied, b * TT + t - 1)
                    for c in range(CT):
                        last = pe.matmul(PV[t % 2][:, :], AT[t % 2][:, c, :], WV[:, c, :], start=(c == 0), stop=(c == CT - 1))
                    last.then_inc(vd_ready, 1)
                for t in range(TT):
                    pe.wait_ge(norm_ready, b * TT + t + 1)
                    pe.wait_ge(copied, b * 2 * TT + TT + t - 1)
                    for c in range(CT):
                        last = pe.transpose(PT[t % 2][:, c, :], XB[:, t, c * P:(c + 1) * P], IDF[:, :])
                    last.then_inc(turned, 1)
                    if t >= 1:
                        values(t - 1)
                values(TT - 1)
                pe.wait_ge(vd_copied, b * TT + TT)

        @block.scalar
        def _(act):
            with act.Fori(0, B) as b:
                for t in range(TT):
                    act.wait_ge(turned, b * 2 * TT + t + 1)
                    if t >= 2:
                        act.wait_ge(y_ready, b * TT + t - 1)
                    nc.scalar.copy(AT[t % 2][:, :, :], PT[t % 2][:, :, :]).then_inc(copied, 1)
                act.wait_ge(var_ready, b + 1)
                nc.scalar.activation(STD[:, :], STD[:, :], ACT.Sqrt).then_inc(std_ready, 1)

                def values(t):
                    act.wait_ge(vd_ready, b * TT + t + 1)
                    if t >= 2:
                        act.wait_ge(vd_out[t % 2], (b * (TT // 2) + t // 2) * 16)
                    nc.scalar.copy(VD[t % 2][:, :], PV[t % 2][:, :]).then_inc(vd_copied, 1)
                act.wait_ge(y_ready, b * TT + TT)
                for t in range(TT):
                    act.wait_ge(turned, b * 2 * TT + TT + t + 1)
                    if t >= 2:
                        act.wait_ge(x1t_ready, b * TT + t - 1)
                        act.wait_ge(vd_ready, b * TT + t - 1)
                    nc.scalar.copy(AT[t % 2][:, :, :], PT[t % 2][:, :, :]).then_inc(copied, 1)
                    if t >= 1:
                        values(t - 1)
                values(TT - 1)
                act.wait_ge(x1t_ready, b * TT + TT)
                for i in range(2):
                    act.wait_ge(vd_out[i], (b + 1) * (TT // 2) * 16)

        @block.vector
        def _(dve):
            with dve.Fori(0, B) as b:
                dve.wait_ge(x_in, b * 16 + 16)
                for t in range(TT):
                    dve.wait_ge(y_ready, b * TT + t + 1)
                    nc.vector.tensor_tensor(XB[:, t, :], PY[t % 2][:, :], XB[:, t, :], ALU.add).then_inc(sum_ready, 1)
                    if t >= 1:
                        dve.wait_ge(sum_ready, b * TT + t)
                        nc.vector.bn_stats(ST[:, t - 1, :], XB[:, t - 1, :]).then_inc(stat_ready, 1)
                dve.wait_ge(sum_ready, b * TT + TT)
                nc.vector.bn_stats(ST[:, TT - 1, :], XB[:, TT - 1, :]).then_inc(stat_ready, 1)
                dve.wait_ge(stat_ready, b * TT + TT)
                nc.vector.memset(MARK[:, :], 0.0)
                for t in range(TT):
                    last = nc.vector.bn_aggr(MV[:, t, :], ST[:, t, :])
                last.then_inc(aggr_ready, 1)
                dve.wait_ge(aggr_ready, b + 1)
                nc.vector.tensor_scalar(STD[:, :], MV[:, :, 1], EPS, None, ALU.add).then_inc(var_ready, 1)
                dve.wait_ge(std_ready, b + 1)
                nc.vector.reciprocal(RSTD[:, :], STD[:, :]).then_inc(rstd_ready, 1)
                dve.wait_ge(rstd_ready, b + 1)
                for t in range(TT):
                    nc.vector.tensor_scalar(XB[:, t, :], XB[:, t, :], MV[:, t, 0:1], RSTD[:, t:t + 1],
                                            ALU.subtract, ALU.mult).then_inc(norm_ready, 1)


def top_tokens(nc, d):
    ctx = ExitStack()
    with ctx:
        sb, pb, sem = scope(nc, ctx)
        X1T, VAL, IDX = d["X1T"], d["VAL"], d["IDX"]
        R = B * DH
        RW = sb("t_rw", [P, CT, B, R], FP32)
        SC = sb("t_sc", [R, T], FP32)
        V8 = sb("t_v8", [R, 8], FP32)
        I8 = sb("t_i8", [R, 8], U32)
        PS = pb("t_ps", [R, T])
        rw_in = sem("t_rw_in")
        score_ready = sem("t_score_ready")
        step = sem("t_step")
        max_ready = sem("t_max_ready")
        taken = sem("t_taken")
        idx_ready = sem("t_idx_ready")
        block = ctx.enter_context(nc.Block())

        @block.sync
        def _(sp):
            sp.dma_start(RW[:, :, :, :], d["router"].rearrange("(c p) b r -> p c b r", p=P)).then_inc(rw_in, 16)

        @block.tensor
        def _(pe):
            pe.wait_ge(rw_in, 16)
            for ch in range(NCH):
                for b in range(B):
                    for c in range(CT):
                        last = pe.matmul(PS[:, ch * CH:(ch + 1) * CH], RW[:, c, b, :],
                                         X1T[:, c, b * T + ch * CH:b * T + (ch + 1) * CH],
                                         start=(b == 0 and c == 0), stop=(b == B - 1 and c == CT - 1))
                last.then_inc(score_ready, 1)

        @block.vector
        def _(dve):
            for ch in range(NCH):
                dve.wait_ge(score_ready, ch + 1)
                nc.vector.tensor_copy(SC[:, ch * CH:(ch + 1) * CH], PS[:, ch * CH:(ch + 1) * CH]).then_inc(step, 1)
            dve.wait_ge(step, NCH)
            with dve.Fori(0, TOP // 8) as k:
                eight = bass.ds(k * 8, 8)
                nc.vector.max(V8[:, :], SC[:, :]).then_inc(max_ready, 1)
                dve.wait_ge(max_ready, k + 1)
                nc.vector.tensor_scalar(VAL[:, eight], V8[:, :], 0.0, None, ALU.add)
                nc.vector.max_index(I8[:, :], V8[:, :], SC[:, :])
                nc.vector.match_replace(SC[:, :], V8[:, :], SC[:, :], -3.0e38).then_inc(taken, 1)
                dve.wait_ge(taken, k + 1)
                nc.vector.tensor_scalar(IDX[:, eight], I8[:, :], 0.0, None, ALU.add).then_inc(idx_ready, 1)
            dve.wait_ge(idx_ready, TOP // 8)


def routed_branch(nc, d):
    ctx = ExitStack()
    with ctx:
        sb, pb, sem = scope(nc, ctx)
        VAL, IDX = d["VAL"], d["IDX"]
        R = B * DH
        KT = TOP // P
        IDF = sb("m_idf", [P, P], FP32)
        ROW0 = sb("m_row0", [P, R], FP32)
        GATE = sb("m_gate", [R, TOP], FP32)
        IG = sb("m_ig", [P, 2, KT, R], FP32)
        OFFF = sb("m_offf", [P, KT, R], FP32)
        OFFX = [sb(f"m_offx{i}", [P, KT], U32) for i in range(2)]
        OFFP = [sb(f"m_offp{i}", [P, KT], U32) for i in range(2)]
        POSG = [sb(f"m_posg{i}", [P, 2, KT], FP32) for i in range(2)]
        XG = [sb(f"m_xg{i}", [P, KT, C], FP32) for i in range(2)]
        CS = [sb(f"m_cs{i}", [P, KT, 2 * ROT], FP32) for i in range(2)]
        WM = [sb(f"m_wm{i}", [P, CT, 3 * DD], FP32) for i in range(2)]
        WO = [sb(f"m_wo{i}", [DD, C], FP32) for i in range(2)]
        KEYP = [sb(f"m_keyp{i}", [P, TOP], FP32) for i in range(2)]
        XGT = sb("m_xgt", [P, CT, TOP], FP32)
        T1 = sb("m_t1", [P, KT, 2, ROT], FP32)
        T2 = sb("m_t2", [P, KT, 2, ROT], FP32)
        QKR = sb("m_qkr", [P, KT, 2, DD], FP32)
        VS = sb("m_vs", [P, KT, DD], FP32)
        QKT = sb("m_qkt", [DD, 2, TOP], FP32)
        MASK = sb("m_mask", [P, KT, TOP], FP32)
        SS = sb("m_ss", [P, KT, TOP], FP32)
        NM = sb("m_nm", [P, 2, KT], FP32)
        DEN = sb("m_den", [P, 3, KT], FP32)
        PR = sb("m_pr", [P, KT, TOP], FP32)
        PRT = sb("m_prt", [P, KT, TOP], FP32)
        AV = sb("m_av", [DD, TOP], FP32)
        Y = [sb(f"m_y{i}", [P, KT, C], FP32) for i in range(2)]
        PX = pb("m_px", [P, CT, TOP])
        PQ = pb("m_pq", [P, KT, C])
        PQT = pb("m_pqt", [DD, 2, TOP])
        PS = pb("m_ps", [P, KT, TOP])
        PP = pb("m_pp", [P, KT, TOP])
        PA = pb("m_pa", [DD, TOP])
        PY = pb("m_py", [P, KT, C])
        gate_exp = sem("m_gate_exp")
        link = sem("m_link")
        gate_ready = sem("m_gate_ready")
        turned = sem("m_turned")
        idx_out = sem("m_idx_out")
        off_ready = sem("m_off_ready")
        go = sem("m_go")
        gathered = [sem(f"m_gathered{i}") for i in range(2)]
        w_in = [sem(f"m_w_in{i}") for i in range(2)]
        xt_ready = sem("m_xt_ready")
        xt_copied = sem("m_xt_copied")
        qkv_ready = sem("m_qkv_ready")
        rot_mul = sem("m_rot_mul")
        rot_ready = sem("m_rot_ready")
        v_copied = sem("m_v_copied")
        qkt_ready = sem("m_qkt_ready")
        qkt_copied = sem("m_qkt_copied")
        s_ready = sem("m_s_ready")
        mask_ready = sem("m_mask_ready")
        ss_ready = sem("m_ss_ready")
        nm_ready = sem("m_nm_ready")
        bias_ready = sem("m_bias_ready")
        p_ready = sem("m_p_ready")
        pt_ready = sem("m_pt_ready")
        pt_copied = sem("m_pt_copied")
        av_ready = sem("m_av_ready")
        av_copied = sem("m_av_copied")
        den_ready = sem("m_den_ready")
        gd_ready = sem("m_gd_ready")
        py_ready = sem("m_py_ready")
        y_ready = sem("m_y_ready")
        added = sem("m_added")
        block = ctx.enter_context(nc.Block())
        PAIRS = DH // 2

        def loop(eng, body):
            with eng.Fori(0, B) as b:
                with eng.Fori(0, PAIRS) as pr:
                    for i in range(2):
                        body(i, b * PAIRS + pr, (b * DH + pr * 2) + i, pr * 2 + i)

        @block.sync
        def _(sp):
            sp.dma_start(d["idxd"], IDX[:, :]).then_inc(idx_out, 16)
            sp.wait_ge(idx_out, 16)
            sp.sem_inc(y_ready, 2)

            def body(i, k, h, n):
                sp.wait_ge(y_ready, h + 1)
                sp.dma_start(WM[i][:, :, :], d["wm"][bass.ds(n, 1), :, :].rearrange("n (c p) f -> p (n c) f", p=P)).then_inc(w_in[i], 16)
                sp.dma_start(WO[i][:, :], d["wmo"][bass.ds(n * DD, DD), :]).then_inc(w_in[i], 16)
                sp.dma_start(KEYP[i][:, :], d["idxd"][bass.ds(h, 1), :].to_broadcast([P, TOP])).then_inc(w_in[i], 16)
            loop(sp, body)

        @block.gpsimd
        def _(pool):
            for dst, name in ((IDF, "ident"), (ROW0, "row0")):
                half = dst.shape[1] // 2
                for part in (slice(0, half), slice(half, 2 * half)):
                    pool.dma_start(dst[:, part], d[name][:, part]).then_inc(added, 16)

            def body(i, k, h, n):
                pool.wait_ge(off_ready, h + 1)
                pool.sem_inc(go, 1)
                for t in range(KT):
                    pool.indirect_dma_start(out=XG[i][:, t, :], out_offset=None, in_=d["x1"],
                                            in_offset=bass.IndirectOffsetOnAxis(ap=OFFX[i][:, t:t + 1], axis=0)).then_inc(gathered[i], 16)
                    pool.indirect_dma_start(out=CS[i][:, t, :], out_offset=None, in_=d["cs64"],
                                            in_offset=bass.IndirectOffsetOnAxis(ap=OFFP[i][:, t:t + 1], axis=0)).then_inc(gathered[i], 16)
                pool.wait_ge(y_ready, h + 3)
                pool.wait_ge(added, h * 32 + 64)
                pool.sem_inc(go, 1)
                for t in range(KT):
                    pool.indirect_dma_start(out=d["y"], out_offset=bass.IndirectOffsetOnAxis(ap=OFFX[i][:, t:t + 1], axis=0),
                                            in_=Y[i][:, t, :], in_offset=None, compute_op=ALU.add).then_inc(added, 16)
            loop(pool, body)
            pool.wait_ge(added, 32 * R + 64)

        @block.tensor
        def _(pe):
            pe.wait_ge(added, 64)
            for t in range(KT):
                pe.matmul(PX[:, 0, t * R:(t + 1) * R], IDX[:, t * P:(t + 1) * P], IDF[0:R, 0:R], start=True, stop=True)
            pe.wait_ge(gate_ready, 1)
            for t in range(KT):
                last = pe.matmul(PX[:, 0, (KT + t) * R:(KT + t + 1) * R], GATE[:, t * P:(t + 1) * P], IDF[0:R, 0:R],
                                 start=True, stop=True)
            last.then_inc(turned, 1)
            pe.wait_ge(link, 4)

            def body(i, k, h, n):
                pe.wait_ge(gathered[i], k * 64 + 64)
                for c in range(CT):
                    for t in range(KT):
                        last = pe.transpose(PX[:, c, t * P:(t + 1) * P], XG[i][:, t, c * P:(c + 1) * P], IDF[:, :])
                last.then_inc(xt_ready, 1)
                pe.wait_ge(w_in[i], k * 48 + 48)
                pe.wait_ge(xt_copied, h + 1)
                for t in range(KT):
                    for c in range(CT):
                        last = pe.matmul(PQ[:, t, 0:3 * DD], XGT[:, c, t * P:(t + 1) * P], WM[i][:, c, :],
                                         start=(c == 0), stop=(c == CT - 1))
                last.then_inc(qkv_ready, 1)
                pe.wait_ge(rot_ready, h + 1)
                pe.wait_ge(v_copied, h + 1)
                for q in range(2):
                    for t in range(KT):
                        last = pe.matmul(PQT[:, q, t * P:(t + 1) * P], QKR[:, t, q, :], IDF[:, :], start=True, stop=True)
                last.then_inc(qkt_ready, 1)
                pe.wait_ge(qkt_copied, h + 1)
                for t in range(KT):
                    last = pe.matmul(PS[:, t, :], QKT[:, 0, t * P:(t + 1) * P], QKT[:, 1, :], start=True, stop=True)
                last.then_inc(s_ready, 1)
                pe.wait_ge(p_ready, h + 1)
                for kt in range(KT):
                    for t in range(KT):
                        last = pe.transpose(PP[:, kt, t * P:(t + 1) * P], PR[:, t, kt * P:(kt + 1) * P], IDF[:, :])
                last.then_inc(pt_ready, 1)
                pe.wait_ge(pt_copied, h + 1)
                for kt in range(KT):
                    last = pe.matmul(PA[:, :], VS[:, kt, :], PRT[:, kt, :], start=(kt == 0), stop=(kt == KT - 1))
                last.then_inc(av_ready, 1)
                pe.wait_ge(av_copied, h + 1)
                for t in range(KT):
                    last = pe.matmul(PY[:, t, :], AV[:, t * P:(t + 1) * P], WO[i][:, :], start=True, stop=True)
                last.then_inc(py_ready, 1)
            loop(pe, body)

        @block.scalar
        def _(act):
            nc.scalar.activation(GATE[:, :], VAL[:, :], ACT.Exp, scale=-1.0).then_inc(gate_exp, 1)

            def body(i, k, h, n):
                act.wait_ge(xt_ready, h + 1)
                nc.scalar.copy(XGT[:, :, :], PX[:, :, :]).then_inc(xt_copied, 1)
                act.wait_ge(qkv_ready, h + 1)
                nc.scalar.copy(QKR[:, :, :, ROT:DD], PQ[:, :, 0:2 * DD].rearrange("p t (q f) -> p t q f", q=2)[:, :, :, ROT:DD])
                nc.scalar.copy(VS[:, :, :], PQ[:, :, 2 * DD:3 * DD]).then_inc(v_copied, 1)
                act.wait_ge(qkt_ready, h + 1)
                nc.scalar.copy(QKT[:, :, :], PQT[:, :, :]).then_inc(qkt_copied, 1)
                act.wait_ge(bias_ready, h + 1)
                for t in range(KT):
                    last = nc.scalar.activation(PR[:, t, :], SS[:, t, :], ACT.Exp, bias=NM[:, 1, t:t + 1], scale=DD ** -0.5,
                                                accum_out=DEN[:, 0, t:t + 1])
                last.then_inc(p_ready, 1)
                act.wait_ge(pt_ready, h + 1)
                nc.scalar.copy(PRT[:, :, :], PP[:, :, :]).then_inc(pt_copied, 1)
                act.wait_ge(av_ready, h + 1)
                nc.scalar.copy(AV[:, :], PA[:, :]).then_inc(av_copied, 1)
            loop(act, body)

        @block.vector
        def _(dve):
            dve.wait_ge(gate_exp, 1)
            nc.vector.tensor_scalar(GATE[:, :], GATE[:, :], 1.0, None, ALU.add).then_inc(link, 1)
            dve.wait_ge(link, 1)
            nc.vector.reciprocal(GATE[:, :], GATE[:, :]).then_inc(gate_ready, 1)
            dve.wait_ge(turned, 1)
            nc.vector.tensor_copy(IG[:, :, :, :].rearrange("p a t r -> p (a t r)"), PX[:, 0, 0:2 * KT * R]).then_inc(link, 1)
            dve.wait_ge(link, 2)
            dve.wait_ge(added, 64)
            nc.vector.tensor_tensor(OFFF[:, :, :], IG[:, 0, :, :], ROW0[:, :].unsqueeze(1).to_broadcast([P, KT, R]), ALU.add).then_inc(link, 1)
            dve.wait_ge(link, 3)
            nc.vector.memset(NM[:, :, :], 0.0).then_inc(link, 1)

            def body(i, k, h, n):
                dve.wait_ge(added, h * 32 + 32)
                row = bass.ds(h, 1)
                nc.vector.tensor_scalar(OFFX[i][:, :].unsqueeze(2), OFFF[:, :, row], 0.0, None, ALU.add)
                nc.vector.tensor_scalar(POSG[i][:, :, :].unsqueeze(3), IG[:, :, :, row], 0.0, None, ALU.add)
                nc.vector.tensor_scalar(OFFP[i][:, :].unsqueeze(2), IG[:, 0, :, row], 0.0, None, ALU.add).then_inc(off_ready, 1)
                dve.wait_ge(w_in[i], k * 48 + 48)
                dve.wait_ge(off_ready, h + 1)
                for t in range(KT):
                    last = nc.vector.tensor_scalar(MASK[:, t, :], KEYP[i][:, :], POSG[i][:, 0, t:t + 1], NEGBIG, ALU.is_gt, ALU.mult)
                last.then_inc(mask_ready, 1)
                dve.wait_ge(v_copied, h + 1)
                dve.wait_ge(gathered[i], k * 64 + 64)
                X = PQ[:, :, 0:2 * DD].rearrange("p t (q f) -> p t q f", q=2)
                H = ROT // 2

                def table(a, b):
                    return CS[i][:, :, a:b].unsqueeze(2).to_broadcast([P, KT, 2, b - a])
                nc.vector.tensor_tensor(T1[:, :, :, :], X[:, :, :, 0:ROT], table(0, ROT), ALU.mult)
                nc.vector.tensor_tensor(T2[:, :, :, 0:H], X[:, :, :, H:ROT], table(ROT, ROT + H), ALU.mult)
                nc.vector.tensor_tensor(T2[:, :, :, H:ROT], X[:, :, :, 0:H], table(ROT + H, 2 * ROT), ALU.mult).then_inc(rot_mul, 1)
                dve.wait_ge(rot_mul, h + 1)
                nc.vector.tensor_tensor(QKR[:, :, :, 0:ROT], T1[:, :, :, :], T2[:, :, :, :], ALU.add).then_inc(rot_ready, 1)
                dve.wait_ge(s_ready, h + 1)
                dve.wait_ge(mask_ready, h + 1)
                nc.vector.tensor_tensor(SS[:, :, :], PS[:, :, :], MASK[:, :, :], ALU.add).then_inc(ss_ready, 1)
                dve.wait_ge(ss_ready, h + 1)
                nc.vector.tensor_reduce(NM[:, 0, :], SS[:, :, :], AX.X, ALU.max, negate=True).then_inc(nm_ready, 1)
                dve.wait_ge(nm_ready, h + 1)
                nc.vector.tensor_scalar(NM[:, 1, :], NM[:, 0, :], DD ** -0.5, None, ALU.mult).then_inc(bias_ready, 1)
                dve.wait_ge(p_ready, h + 1)
                nc.vector.reciprocal(DEN[:, 1, :], DEN[:, 0, :]).then_inc(den_ready, 1)
                dve.wait_ge(den_ready, h + 1)
                nc.vector.tensor_tensor(DEN[:, 2, :], DEN[:, 1, :], POSG[i][:, 1, :], ALU.mult).then_inc(gd_ready, 1)
                dve.wait_ge(gd_ready, h + 1)
                dve.wait_ge(py_ready, h + 1)
                for t in range(KT):
                    last = nc.vector.tensor_scalar(Y[i][:, t, :], PY[:, t, :], DEN[:, 2, t:t + 1], None, ALU.mult)
                last.then_inc(y_ready, 1)
            loop(dve, body)


PIECES = 4
GROUP = 4
ESLOTS = 3
DUNITS = TT // 2 + TT


def dense_branch(nc, d, out):
    ctx = ExitStack()
    with ctx:
        sb, pb, sem = scope(nc, ctx)
        X1T = d["X1T"]
        COS = sb("d_cos", [P, T], FP32)
        SIN = sb("d_sin", [P, T], FP32)
        IDF = sb("d_idf", [P, P], FP32)
        IDB = sb("d_idb", [P, P], BF16)
        NEGQ = sb("d_negq", [P, P], BF16)
        NEGK = sb("d_negk", [P, P], BF16)
        WO = sb("d_wo", [P, DH * DD // P, C], FP32)
        W = [sb(f"d_w{i}", [P, CT, 4 * DD], FP32) for i in range(2)]
        Q = [sb(f"d_q{i}", [DD + 1, T], FP32) for i in range(2)]
        K = [sb(f"d_k{i}", [DD + 1, T], FP32) for i in range(2)]
        KK = sb("d_kk", [P, T], FP32)
        V = [sb(f"d_v{i}", [P, TT, P], FP32) for i in range(2)]
        E = sb("d_e", [P, ESLOTS, HALF], FP32)
        AV = sb("d_av", [P, DH // 2, T], FP32)
        RD = sb("d_rd", [P, HALF], FP32)
        T1 = sb("d_t1", [P, 2, CH], FP32)
        T2 = sb("d_t2", [P, 2, CH], FP32)
        MX = sb("d_mx", [P, TT, NCH], FP32)
        NEG = sb("d_neg", [P, P], FP32)
        MT = sb("d_mt", [TT, P], FP32)
        ST = sb("d_st", [P, TT, 6], FP32)
        MV = sb("d_mv", [P, TT, 4], FP32)
        POW = sb("d_pow", [P, GROUP, 1], FP32)
        MARK = sb("d_mark", [P, 1], FP32)
        PS = [pb(f"d_ps{i}", [P, HALF]) for i in range(2)]
        PO = pb("d_po", [P, HALF])
        PM = [pb(f"d_pm{i}", [P, CH]) for i in range(2)]
        const_in = sem("d_const_in")
        init = sem("d_init")
        w_in = [sem(f"d_w_in{i}") for i in range(2)]
        v_in = [sem(f"d_v_in{i}") for i in range(2)]
        k_in = [sem(f"d_k_in{i}") for i in range(2)]
        m_in = sem("d_m_in")
        y_in = sem("d_y_in")
        y_out = sem("d_y_out")
        ring_ready = sem("d_ring_ready")
        ring_read = sem("d_ring_read")
        qk_sum = sem("d_qk_sum")
        neg_ready = sem("d_neg_ready")
        s_ready = sem("d_s_ready")
        e_ready = sem("d_e_ready")
        av_ready = sem("d_av_ready")
        av_raw = sem("d_av_raw")
        rd_ready = sem("d_rd_ready")
        inv_ready = sem("d_inv_ready")
        rd_go = sem("d_rd_go")
        av_out = sem("d_av_out")
        st_ready = sem("d_st_ready")
        aggr_ready = sem("d_aggr_ready")
        var_ready = sem("d_var_ready")
        std_ready = sem("d_std_ready")
        o_ready = sem("d_o_ready")
        init2 = sem("d_init2")
        RING = 2 * NCH + sum(t // NCH + 1 for t in range(TT)) + 1

        def unit(u):
            half, j = (0, u) if u < TT // 2 else (1, u - TT // 2)
            return half, j, max(0, j * P - half * HALF)

        def pieces(x0):
            return [(a, b) for a, b in ((x0, CH), (max(x0, CH), HALF)) if a < b]

        def ahead(e):
            todo = []
            for ch in range(NCH):
                todo += [("product", e, 2 * ch), ("product", e, 2 * ch + 1)]
            todo.append(("keys", e, 0))
            for t in range(TT):
                todo += [("chunk", e, t * NCH + c) for c in range(t // NCH + 1)]
            todo.append(("turn", e, 0))
            return todo
        RINGK = ("product", "chunk", "turn", "out")
        PROJECTED, CHUNKED, TURNED = 4, DUNITS - 5, DUNITS - 4

        def due(todo, u):
            keys, turn = 2 * NCH + 1, len(todo) - 1
            if u <= PROJECTED:
                return keys * u // PROJECTED
            if u <= CHUNKED:
                return keys + (turn - keys) * (u - PROJECTED - 1) // (CHUNKED - PROJECTED - 1)
            return turn if u < TURNED else len(todo)

        def pair_steps(more, closing=False):
            out = []
            for e in range(2):
                todo = ahead(e + 1) if e == 0 or more else []
                if e == 0 or more:
                    out.append(("values_in", e + 1, 0))
                if e == 1 and closing:
                    out.append(("y_in", 0, 0))
                if more:
                    out.append(("weights_in", e + 2, 0))
                done = 0
                for u in range(DUNITS):
                    out.append(("scores", e, u))
                    if TT // 2 < u <= TT // 2 + PIECES:
                        out.append(("inverse", e, u - TT // 2 - 1))
                    want = due(todo, u) if todo else 0
                    out += todo[done:want]
                    done = want
                    if u >= 1:
                        out.append(("values", e, u - 1))
                out.append(("values", e, DUNITS - 1))
                out += [("inverse", e, PIECES + piece) for piece in range(PIECES)]
            return out

        def run(engine, step):
            def walk(steps, b, pr, ring, h):
                n = dict(ring=ring, scores=h * DUNITS, values=h * DUNITS, par=1, b=b, pr=pr, h=h)
                for s in steps:
                    step(s, n)
                    if s[0] in RINGK:
                        n["par"] ^= 1
                        n["ring"] = n["ring"] + 1
                    elif s[0] in ("scores", "values"):
                        n[s[0]] = n[s[0]] + 1

            def ring_at(b, pr):
                return b * (DH * RING + TT) + pr * (2 * RING) + RING

            def batch(b, last):
                with engine.Fori(0, DH // 2 - 1) as pr:
                    walk(pair_steps(True), b, pr, ring_at(b, pr), b * DH + pr * 2)
                pr = DH // 2 - 1
                walk(pair_steps(not last, True), b, pr, ring_at(b, pr), b * DH + pr * 2)
                ring = ring_at(b, pr) + (RING if last else 2 * RING)
                n = dict(ring=ring, par=0 if last else 1, b=b, pr=DH // 2, h=b * DH + DH)
                for t in range(TT):
                    step(("out", 0, t), n)
                    n["par"] ^= 1
                    n["ring"] = n["ring"] + 1
                step(("out_end", 0, TT), n)
            n = dict(ring=0, par=0, b=0, pr=0, h=0)
            for s in [("values_in", 0, 0), ("weights_in", 0, 0), ("weights_in", 1, 0)] + ahead(0):
                step(s, n)
                if s[0] in RINGK:
                    n["par"] ^= 1
                    n["ring"] += 1
            assert n["ring"] == RING and RING % 2 == 1
            with engine.Fori(0, B - 1) as b:
                batch(b, False)
            batch(B - 1, True)

        block = ctx.enter_context(nc.Block())

        @block.sync
        def _(sp):
            for dst, name in ((COS, "cos64"), (SIN, "sin64"), (IDF, "ident"), (IDB, "ident_bf16"), (NEGQ, "negq"), (NEGK, "negk")):
                sp.dma_start(dst[:, :], d[name]).then_inc(const_in, 16)
            sp.dma_start(WO[:, :, :], d["wdo"].rearrange("(k p) c -> p k c", p=P)).then_inc(const_in, 16)
            sp.wait_ge(init, 5)

            def step(s, n):
                kind, e, k = s
                h, b = n["h"], n["b"]
                if kind == "weights_in":
                    sp.dma_start(W[e % 2][:, :, :], d["wd"][bass.ds(n["pr"] * 2 + e, 1), :, :]
                                 .rearrange("n (c p) f -> p (n c) f", p=P)).then_inc(w_in[e % 2], 16)
                elif kind == "values_in":
                    if n.get("scores") is not None:
                        sp.wait_ge(av_ready, (h + e - 1) * DUNITS + ESLOTS)
                    sp.dma_start(V[e % 2][:, :, e % 2 * DD:(e % 2 + 1) * DD], d["vd"][bass.ds(h + e, 1), :, :, :]
                                 .rearrange("n p t f -> p (n t) f")).then_inc(v_in[e % 2], 16)
                elif kind == "keys":
                    sp.wait_ge(qk_sum, (h + e + 1) * NCH + 2)
                    sp.dma_start(K[e % 2][0:DD, :], KK[DD:P, :]).then_inc(k_in[e % 2], 16)
                elif kind == "turn":
                    sp.wait_ge(ring_read, n["ring"] + 3)
                    sp.dma_start(Q[e % 2][DD:DD + 1, :], MT[:, :]).then_inc(m_in, 16)
                elif kind == "y_in":
                    sp.wait_ge(qk_sum, (h + 2) * NCH + 2)
                    for c in range(CT):
                        sp.dma_start(X1T[:, c, bass.ds(b * T, T)].rearrange("p (t c) -> p t c", c=C),
                                     d["y"][bass.ds(b * T + c * HALF, HALF), :].rearrange("(t p) c -> p t c", p=P)).then_inc(y_in, 16)
                elif kind == "out" and k % GROUP == 0 and k > GROUP:
                    store(b, k // GROUP - 2)
                elif kind == "out_end":
                    for g in (TT // GROUP - 2, TT // GROUP - 1):
                        store(b, g)

            def store(b, g):
                sp.wait_ge(o_ready, b * TT + (g + 1) * GROUP)
                c, t = g * GROUP // (TT // CT), g * GROUP % (TT // CT)
                sp.dma_start(out[bass.ds(b, 1), g * GROUP * P:(g + 1) * GROUP * P, :].rearrange("b (t p) c -> p (b t) c", p=P),
                             X1T[:, c, bass.ds(b * T + t * C, GROUP * C)].rearrange("p (t c) -> p t c", c=C)).then_inc(y_out, 16)
            run(sp, step)
            sp.wait_ge(y_out, B * TT // GROUP * 16)

        @block.gpsimd
        def _(pool):
            for i in range(2):
                nc.gpsimd.memset(K[i][DD:DD + 1, :], 1.0).then_inc(init, 1)
                pool.wait_ge(init, 2 * i + 1)
                nc.gpsimd.memset(V[i][:, :, (1 - i) * DD:(2 - i) * DD], 1.0).then_inc(init, 1)
                pool.wait_ge(init, 2 * i + 2)
            nc.gpsimd.memset(POW[:, :, :], -0.5).then_inc(init, 1)
            pool.sem_inc(qk_sum, 2)
            pool.sem_inc(av_out, 1)
            pool.sem_inc(m_in, 16)
            for t in range(2):
                pool.sem_inc(k_in[t], 16)

            def step(s, n):
                kind, e, k = s
                h = n["h"]
                if kind == "product" and k % 2 == 1:
                    ch = k // 2
                    hh = h + e
                    pool.wait_ge(ring_read, n["ring"] + 3)
                    if ch == 0:
                        if e >= 1:
                            pool.wait_ge(av_ready, (hh - 1) * DUNITS + ESLOTS)
                            pool.wait_ge(k_in[(e + 1) % 2], (n["b"] * (DH // 2) + n["pr"] + 1) * 16 + 16)
                    cols = slice(ch * CH, (ch + 1) * CH)
                    nc.gpsimd.tensor_tensor(Q[e % 2][0:DD, cols], T1[0:DD, ch % 2, :], T2[0:DD, ch % 2, :], ALU.add)
                    nc.gpsimd.tensor_tensor(KK[DD:P, cols], T1[DD:P, ch % 2, :], T2[DD:P, ch % 2, :], ALU.add).then_inc(qk_sum, 1)
                elif kind == "inverse" and k % PIECES == PIECES - 1:
                    half = k // PIECES
                    pool.wait_ge(av_raw, (h + e) * 2 + half + 2)
                    pool.wait_ge(inv_ready, (h + e) * 2 + half + 1)
                    pool.sem_inc(rd_go, 1)
                    mine = slice(e * DD, (e + 1) * DD)
                    part = AV[mine, bass.ds(n["pr"], 1), half * HALF:(half + 1) * HALF]
                    nc.gpsimd.tensor_tensor(part, part, RD[mine, :].unsqueeze(1), ALU.mult).then_inc(av_out, 1)
                elif kind == "out" and k % GROUP == GROUP - 1:
                    pool.wait_ge(var_ready, n["b"] * (TT // GROUP) + k // GROUP + 1)
                    group = MV[:, k - GROUP + 1:k + 1, :]
                    nc.gpsimd.tensor_tensor(group[:, :, 3:4], group[:, :, 2:3], POW[:, :, :], ALU.pow).then_inc(std_ready, 1)

            run(pool, step)

        @block.tensor
        def _(pe):
            pe.wait_ge(const_in, 16 * 7)
            pe.wait_ge(init, 5)
            pe.sem_inc(av_ready, ESLOTS)

            def step(s, n):
                kind, e, k = s
                h, b, pr = n["h"], n["b"], n["pr"]
                h2 = b * (DH // 2) + pr
                if kind in RINGK:
                    pe.wait_ge(ring_read, n["ring"] + 1)
                    pm = PM[n["par"]]
                if kind == "product":
                    if k == 0:
                        pe.wait_ge(w_in[e % 2], (h2 + e // 2 + 1) * 16)
                    ch, w = k // 2, k % 2
                    bb = b + 1 if isinstance(pr, int) and pr == DH // 2 - 1 and e == 2 else b
                    for c in range(CT):
                        last = pe.matmul(pm[:, :], W[e % 2][:, c, w * P:(w + 1) * P], X1T[:, c, bass.ds(bb * T + ch * CH, CH)],
                                         start=(c == 0), stop=(c == CT - 1))
                    last.then_inc(ring_ready, 1)
                elif kind == "chunk":
                    t, c = k // NCH, k % NCH
                    if t == 0:
                        pe.wait_ge(qk_sum, (h + e + 1) * NCH + 2)
                        pe.wait_ge(k_in[e % 2], (h2 + e // 2 + 1) * 16 + 16)
                    w = min(CH, (t + 1) * P - c * CH)
                    diag = c == t // NCH
                    last = pe.matmul(pm[:, 0:w], Q[e % 2][0:DD, t * P:(t + 1) * P], K[e % 2][0:DD, c * CH:c * CH + w],
                                     start=True, stop=not diag)
                    if diag:
                        last = pe.matmul(pm[:, w - P:w], IDB[:, :], NEGQ[:, :], start=False, stop=True)
                    last.then_inc(ring_ready, 1)
                elif kind == "turn":
                    pe.wait_ge(neg_ready, h + e + 1)
                    pe.transpose(pm[:, 0:P], NEG[:, :], IDF[:, :]).then_inc(ring_ready, 1)
                elif kind == "scores":
                    half, j, x0 = unit(k)
                    if k == 0:
                        pe.wait_ge(m_in, (h + e + 1) * 16 + 16)
                    pe.wait_ge(e_ready, n["scores"] + 1)
                    diag = j * P >= half * HALF
                    for a, z in pieces(x0):
                        own = diag and a == x0
                        last = pe.matmul(PS[k % 2][:, a:z], K[e][:, j * P:(j + 1) * P], Q[e][:, half * HALF + a:half * HALF + z],
                                         start=True, stop=not own)
                        if own:
                            last = pe.matmul(PS[k % 2][:, x0:x0 + P], IDB[:, :], NEGK[:, :], start=False, stop=True)
                    last.then_inc(s_ready, 1)
                elif kind == "values":
                    half, j, x0 = unit(k)
                    if k == 0:
                        pe.wait_ge(v_in[e], (h2 + 1) * 16)
                    pe.wait_ge(e_ready, n["values"] + 3)
                    if j == 0:
                        pe.wait_ge(av_raw, (h + e) * 2 + half + 1)
                        pe.wait_ge(rd_ready, (h + e) * 2 + half + 1)
                    for a, z in pieces(x0):
                        end = (half * HALF + z) // P - 1
                        last = pe.matmul(PO[:, a:z], V[e][:, j, :], E[:, k % ESLOTS, a:z], start=(j == 0), stop=(j == end))
                    last.then_inc(av_ready, 1)
                elif kind == "out":
                    if k == 0:
                        pe.wait_ge(av_out, h * 2 + 1)
                    for kt in range(DH // 2):
                        last = pe.matmul(pm[:, 0:C], AV[:, kt, k * P:(k + 1) * P], WO[:, kt, :],
                                         start=(kt == 0), stop=(kt == DH // 2 - 1))
                    last.then_inc(ring_ready, 1)
            run(pe, step)

        @block.scalar
        def _(act):
            act.sem_inc(e_ready, 2)
            act.sem_inc(rd_ready, 1)

            def step(s, n):
                kind, e, k = s
                if kind == "scores":
                    _, _, x0 = unit(k)
                    act.wait_ge(s_ready, n["scores"] + 1)
                    act.wait_ge(av_ready, n["scores"] + 1)
                    nc.scalar.activation(E[:, k % ESLOTS, x0:HALF], PS[k % 2][:, x0:HALF], ACT.Exp,
                                         scale=DD ** -0.5).then_inc(e_ready, 1)
                elif kind == "values":
                    half, j, _ = unit(k)
                    if j == (half + 1) * (TT // 2) - 1:
                        hh = n["h"] + e
                        act.wait_ge(av_ready, n["values"] + 1 + ESLOTS)
                        act.wait_ge(av_out, hh * 2 + half + 1)
                        nc.scalar.copy(RD[e * DD:(e + 1) * DD, :], PO[(1 - e) * DD:(2 - e) * DD, :]).then_inc(rd_ready, 1)
            run(act, step)

        @block.vector
        def _(dve):
            nc.vector.memset(MX[:, :, :], -3.0e38).then_inc(init2, 1)
            nc.vector.memset(NEG[:, :], 0.0).then_inc(init2, 1)
            dve.sem_inc(ring_read, 2)
            dve.sem_inc(av_raw, 1)
            dve.wait_ge(const_in, 16 * 7)
            dve.wait_ge(init2, 2)

            def step(s, n):
                kind, e, k = s
                h, b, pr = n["h"], n["b"], n["pr"]
                if kind in RINGK:
                    dve.wait_ge(ring_ready, n["ring"] + 1)
                    pm = PM[n["par"]]
                if kind == "product":
                    ch = k // 2
                    if k % 2 == 0:
                        dve.wait_ge(qk_sum, (h + e) * NCH + ch + 1)
                    nc.vector.tensor_tensor((T1 if k % 2 == 0 else T2)[:, ch % 2, :], pm[:, :],
                                            (COS if k % 2 == 0 else SIN)[:, ch * CH:(ch + 1) * CH], ALU.mult).then_inc(ring_read, 1)
                elif kind == "chunk":
                    t, c = k // NCH, k % NCH
                    w = min(CH, (t + 1) * P - c * CH)
                    nc.vector.reduce_max(MX[:, t, c:c + 1], pm[:, 0:w], AX.X).then_inc(ring_read, 1)
                    if k == TT * NCH - 1:
                        dve.wait_ge(ring_read, n["ring"] + 3)
                        nc.vector.tensor_reduce(NEG[:, 0:TT], MX[:, :, :], AX.X, ALU.max, negate=True).then_inc(neg_ready, 1)
                elif kind == "turn":
                    dve.wait_ge(m_in, (h + e) * 16 + 16)
                    nc.vector.tensor_copy(MT[:, :], pm[0:TT, 0:P]).then_inc(ring_read, 1)
                elif kind == "values":
                    half, j, _ = unit(k)
                    if j == (half + 1) * (TT // 2) - 1:
                        dve.wait_ge(av_ready, n["values"] + 1 + ESLOTS)
                        mine = slice(e * DD, (e + 1) * DD)
                        nc.vector.tensor_copy(AV[mine, bass.ds(pr, 1), half * HALF:(half + 1) * HALF],
                                              PO[mine, :].unsqueeze(1)).then_inc(av_raw, 1)
                elif kind == "inverse":
                    half, piece = k // PIECES, k % PIECES
                    if piece == 0:
                        dve.wait_ge(rd_ready, (h + e) * 2 + half + 2)
                    part = RD[e * DD:(e + 1) * DD, piece * HALF // PIECES:(piece + 1) * HALF // PIECES]
                    last = nc.vector.reciprocal(part, part)
                    if piece == PIECES - 1:
                        last.then_inc(inv_ready, 1)
                elif kind == "out":
                    if k == 0:
                        dve.wait_ge(y_in, (b + 1) * 32)
                    nc.vector.tensor_tensor(tile(b, k), pm[:, 0:C], tile(b, k), ALU.add).then_inc(ring_read, 1)
                    if k > GROUP:
                        norm(b, k - GROUP - 1)
                    dve.wait_ge(ring_read, n["ring"] + 3)
                    nc.vector.memset(MARK[:, :], 0.0)
                    nc.vector.bn_stats(ST[:, k, :], tile(b, k)).then_inc(st_ready, 1)
                    if k % GROUP == GROUP - 1:
                        dve.wait_ge(st_ready, b * TT + k + 1)
                        nc.vector.memset(MARK[:, :], 0.0)
                        for t in range(k - GROUP + 1, k + 1):
                            last = nc.vector.bn_aggr(MV[:, t, 0:2], ST[:, t, :])
                        last.then_inc(aggr_ready, 1)
                        dve.wait_ge(aggr_ready, b * (TT // GROUP) + k // GROUP + 1)
                        group = MV[:, k - GROUP + 1:k + 1, :]
                        nc.vector.tensor_scalar(group[:, :, 2:3], group[:, :, 1:2], EPS, None, ALU.add).then_inc(var_ready, 1)
                elif kind == "out_end":
                    for t in range(TT - GROUP - 1, TT):
                        norm(b, t)

            def tile(b, t):
                return X1T[:, t // (TT // CT), bass.ds(b * T + t % (TT // CT) * C, C)]

            def norm(b, t):
                dve.wait_ge(std_ready, b * (TT // GROUP) + t // GROUP + 1)
                nc.vector.tensor_scalar(tile(b, t), tile(b, t), MV[:, t, 0:1], MV[:, t, 3:4],
                                        ALU.subtract, ALU.mult).then_inc(o_ready, 1)
            run(dve, step)


def kernel_program(nc, d, out):
    with nc.sbuf_tensor("x1t", [P, CT, B * T], FP32) as X1T:
        d["X1T"] = X1T
        project_attention(nc, d)
        with nc.sbuf_tensor("att", [P, NBH * TT, HD], FP32) as ATT:
            d["ATT"] = ATT
            full_attention(nc, d)
            first_norm(nc, d)
        with (nc.sbuf_tensor("val", [B * DH, TOP], FP32) as VAL, nc.sbuf_tensor("idx", [B * DH, TOP], FP32) as IDX):
            d.update(VAL=VAL, IDX=IDX)
            top_tokens(nc, d)
            routed_branch(nc, d)
        dense_branch(nc, d, out)


def swap_halves(a, width, half):
    import numpy as np
    heads = a.reshape((-1, width) + a.shape[1:])
    parts = [heads[:, half:2 * half], heads[:, 0:half], heads[:, 2 * half:]]
    return np.concatenate(parts, axis=1).reshape(a.shape)


def rotation(inv, length, width):
    import numpy as np
    half = len(inv)
    ang = (np.arange(length, dtype=np.float32)[None, :] * inv[:, None]).astype(np.float32)
    cos, sin = np.cos(ang).astype(np.float32), np.sin(ang).astype(np.float32)
    rest = width - 2 * half
    c = np.concatenate([cos, cos, np.ones((rest, length), np.float32)])
    s = np.concatenate([-sin, sin, np.zeros((rest, length), np.float32)])
    return c, s


def kernel(**inputs):
    import numpy as np
    import ml_dtypes
    import concourse.bacc as bacc
    from concourse.bass_utils import run_bass_kernel_spmd
    nc = bacc.Bacc("TRN2", target_bir_lowering=False, num_devices=1)
    x = np.asarray(inputs["L0_attn_x"])
    W = {k: np.asarray(inputs["L0_attn_W" + k]) for k in "qkvo"}
    bias = {k: np.asarray(inputs["L0_attn_b" + k]) for k in "qkvo"}

    def swapped(a):
        return swap_halves(a, HD, HD // 2)
    cols = [W["q"], swapped(W["q"]), W["k"], swapped(W["k"]), W["v"]]
    bcol = [bias["q"], swapped(bias["q"]), bias["k"], swapped(bias["k"])]
    base = np.float32(10000.0)
    cos16, sin16 = rotation(1.0 / base ** (np.arange(0, HD, 2, dtype=np.float32) / HD), T, HD)
    cos32, sin32 = rotation(base ** (-np.arange(ROT // 2, dtype=np.float32) / (ROT // 2)), T, DD)
    sel = np.zeros((P, HD + 1), np.float32)
    for g in range(4):
        for f in range(HD + 1):
            sel[g * VW + f, f] = 1.0
    router = np.asarray(inputs["L0_ffn_mosa_router_w"])
    routed = np.zeros((C, B, B * DH), np.float32)
    for b in range(B):
        routed[:, b, b * DH:(b + 1) * DH] = router
    wd = np.asarray(inputs["L0_ffn_dense_wqkv"])
    plain = [wd[:, :, 0:DD], wd[:, :, DD:2 * DD]]
    swap = [swap_halves(w.transpose(1, 2, 0).reshape(DH * DD, C), DD, ROT // 2).reshape(DH, DD, C).transpose(2, 0, 1) for w in plain]
    wd4 = np.concatenate(plain + swap, axis=2).transpose(1, 0, 2)
    wd4 = np.concatenate([wd4, wd4[0:2]], axis=0)
    after = np.triu(np.full((P, P), NEGBIG, np.float32), 1)
    arrays = {
        "x": x,
        "xT": x.transpose(0, 2, 1),
        "wqkv": np.stack([w.T for w in cols], axis=1),
        "bqk": np.stack(bcol).reshape(4, CT, P).transpose(2, 0, 1),
        "bv": bias["v"][None, :],
        "cos16": np.tile(cos16, (P // HD, 1)),
        "sin16": np.tile(sin16, (P // HD, 1)),
        "sel17": sel,
        "woT": W["o"].T,
        "bo": bias["o"][None, :],
        "ident": np.eye(P, dtype=np.float32),
        "wdv": np.asarray(inputs["L0_ffn_dense_wqkv"])[:, :, 2 * DD:].reshape(C, DH * DD),
        "wd": wd4,
        "wdo": np.asarray(inputs["L0_ffn_dense_wo"]),
        "cos64": np.tile(cos32, (2, 1)),
        "sin64": np.tile(sin32, (2, 1)),
        "negq": after.astype(ml_dtypes.bfloat16),
        "negk": after.T.astype(ml_dtypes.bfloat16),
        "router": routed,
        "row0": np.broadcast_to((np.arange(B * DH) // DH * T).astype(np.float32), (P, B * DH)),
        "cs64": np.concatenate([cos32[:ROT].T, sin32[:ROT].T], axis=1),
        "wm": np.asarray(inputs["L0_ffn_mosa_wqkv"]).transpose(1, 0, 2),
        "wmo": np.asarray(inputs["L0_ffn_mosa_wo"]),
        "ident_bf16": np.eye(P).astype(ml_dtypes.bfloat16),
    }
    arrays = {k: np.ascontiguousarray(v) for k, v in arrays.items()}
    d = {k: nc.dram_tensor("in_" + k, v.shape, mybir.dt.from_np(v.dtype), kind="ExternalInput").ap() for k, v in arrays.items()}
    for name, shape, dt in (("qs", (PARTS, B * C, T), BF16), ("ks", (PARTS, B * C, T), BF16), ("vs", (NBH, P, TT * VW), FP32),
                            ("idxd", (B * DH, TOP), FP32), ("x1", (B * T, C), FP32), ("y", (B * T, C), FP32), ("vd", (B * DH, P, TT, DD), FP32)):
        d[name] = nc.dram_tensor("scratch_" + name, shape, dt).ap()
    out = nc.dram_tensor("out", (B, T, C), FP32, kind="ExternalOutput").ap()
    kernel_program(nc, d, out)
    got = run_bass_kernel_spmd(nc, [{"in_" + k: v for k, v in arrays.items()}], core_ids=[0])
    return got.results[0]["out"]
```

```python
import concourse.bass as bass
from concourse import mybir
from contextlib import ExitStack

FP32 = mybir.dt.float32
BF16 = mybir.dt.bfloat16
U32 = mybir.dt.uint32
ALU = mybir.AluOpType
ACT = mybir.ActivationFunctionType
AX = mybir.AxisListType

P = 128
B, T, C = 4, 2048, 256
HEADS, HD = 16, 16
CT = C // P
TT = T // P
CH = 512
NCH = T // CH
NBH = B * HEADS
VW = 32
PARTS = 3
STACK = 6 * HD
MROWS = 3
HALF = T // 2


def scope(nc, ctx):
    def sb(name, shape, dt):
        return ctx.enter_context(nc.sbuf_tensor(name, shape, dt))

    def pb(name, shape, dt=FP32):
        return ctx.enter_context(nc.psum_tensor(name, shape, dt))

    def sem(name):
        return ctx.enter_context(nc.semaphore(name))
    return sb, pb, sem


ASLOTS = 4


def project_attention(nc, d):
    ctx = ExitStack()
    with ctx:
        sb, pb, sem = scope(nc, ctx)
        XT = [sb(f"a_xT{i}", [P, CT, T], FP32) for i in range(2)]
        W = sb("a_w", [P, CT, 3, C], FP32)
        BIAS = sb("a_bias", [P, 4, CT], FP32)
        BV = sb("a_bv", [1, C], FP32)
        ONES = sb("a_ones", [1, P], FP32)
        COS = sb("a_cos", [P, T], FP32)
        SIN = sb("a_sin", [P, T], FP32)
        T1 = sb("a_t1", [P, 2, CH], FP32)
        T2 = sb("a_t2", [P, 2, CH], FP32)
        F = sb("a_f", [P, 2, CH], FP32)
        R = sb("a_r", [P, 2, CH], FP32)
        S = [sb(f"a_s{i}", [P, PARTS, T], BF16) for i in range(2)]
        V = sb("a_v", [P, HEADS, TT, VW], FP32)
        PA = [pb(f"a_pa{i}", [P, CH]) for i in range(ASLOTS)]
        PV = [pb(f"a_pv{i}", [P, CH]) for i in range(2)]
        const_in = sem("a_const_in")
        x_in = [sem(f"a_x_in{i}") for i in range(2)]
        v_init = sem("a_v_init")
        xt_free = sem("a_xt_free")
        qk_ready = sem("a_qk_ready")
        qk_read = sem("a_qk_read")
        rot_ready = sem("a_rot_ready")
        f_ready = sem("a_f_ready")
        hi_ready = sem("a_hi_ready")
        r_ready = sem("a_r_ready")
        mid_ready = sem("a_mid_ready")
        lo_ready = sem("a_lo_ready")
        s_out = [sem(f"a_s_out{i}") for i in range(2)]
        v_ready = sem("a_v_ready")
        v_copied = sem("a_v_copied")
        v_out = sem("a_v_out")
        G = 2 * CT * NCH
        SWAP = [lane // HD * HD + (lane + HD // 2) % HD for lane in range(32)]
        block = ctx.enter_context(nc.Block())

        @block.sync
        def _(sp):
            sp.dma_start(W[:, :, :, :], d["wqkv"].rearrange("(c p) w o -> p c w o", p=P)).then_inc(const_in, 16)
            sp.dma_start(BIAS[:, :, :], d["bqk"]).then_inc(const_in, 16)
            sp.dma_start(BV[:, :], d["bv"]).then_inc(const_in, 16)
            sp.dma_start(COS[:, :], d["cos16"]).then_inc(const_in, 16)
            sp.dma_start(SIN[:, :], d["sin16"]).then_inc(const_in, 16)
            with sp.Fori(0, B // 2) as bb:
                for i in range(2):
                    sp.wait_ge(xt_free, bb * 2 + 1)
                    sp.dma_start(XT[i][:, :, :], d["xT"][bass.ds(bb * 2 + i, 1)].rearrange("b (c p) t -> p (b c) t", p=P)).then_inc(x_in[i], 16)
                for i in range(2):
                    b = bb * 2 + i
                    for tile in range(2 * CT):
                        qk, ot = tile // CT, tile % CT
                        sp.wait_ge(lo_ready, b * G + (tile + 1) * NCH)
                        sp.dma_start(d["qs" if qk == 0 else "ks"][:, bass.ds(b * C + ot * P, P), :]
                                     .rearrange("s p t -> p s t"), S[tile % 2][:, :, :]).then_inc(s_out[tile % 2], 16)
                    sp.wait_ge(v_copied, (b + 1) * TT)
                    sp.dma_start(d["vs"][bass.ds(b * HEADS, HEADS), :, :].rearrange("h p f -> p h f"),
                                 V[:, :, :, :].rearrange("p h t f -> p h (t f)")).then_inc(v_out, 16)
            for i in range(2):
                sp.wait_ge(s_out[i], 16 * CT * B)
            sp.wait_ge(v_out, 16 * B)

        @block.gpsimd
        def _(pool):
            nc.gpsimd.memset(V[:, :, :, :], 0.0).then_inc(v_init, 1)
            pool.wait_ge(v_init, 1)
            nc.gpsimd.memset(V[:, :, :, HD:HD + 1], 1.0).then_inc(v_init, 1)
            nc.gpsimd.memset(ONES[:, :], 1.0).then_inc(v_init, 1)
            pool.sem_inc(xt_free, 1)
            pool.sem_inc(f_ready, 2)
            with pool.Fori(0, B // 2) as bb:
                for i in range(2):
                    b = bb * 2 + i

                    def rest(g):
                        tile, ch = g // NCH, g % NCH
                        pool.wait_ge(hi_ready, b * G + g + 1)
                        if g >= 2 or i >= 1:
                            pool.wait_ge(lo_ready, b * G + g - 1)
                        nc.gpsimd.tensor_tensor(R[:, g % 2, :], F[:, g % 2, :],
                                                S[tile % 2][:, 0, ch * CH:(ch + 1) * CH], ALU.subtract).then_inc(r_ready, 1)

                    for g in range(G):
                        pool.wait_ge(rot_ready, b * G + g + 1)
                        if g >= 2 or i >= 1:
                            pool.wait_ge(r_ready, b * G + g - 1)
                        nc.gpsimd.tensor_tensor(F[:, g % 2, :], T1[:, g % 2, :], T2[:, g % 2, :], ALU.add).then_inc(f_ready, 1)
                        if g >= 1:
                            rest(g - 1)
                    rest(G - 1)
                pool.wait_ge(lo_ready, bb * (2 * G) + 2 * G)
                pool.wait_ge(v_ready, bb * (2 * TT) + 2 * TT)
                pool.sem_inc(xt_free, 2)

        @block.tensor
        def _(pe):
            pe.wait_ge(const_in, 16 * 5)
            pe.wait_ge(v_init, 3)
            with pe.Fori(0, B // 2) as bb:
                for i in range(2):
                    b = bb * 2 + i
                    pe.wait_ge(x_in[i], bb * 16 + 16)
                    for g in range(G):
                        qk, ot, ch = g // (CT * NCH), (g // NCH) % CT, g % NCH
                        if g >= ASLOTS or i >= 1:
                            pe.wait_ge(qk_read, b * G + g - ASLOTS + 1)
                        for c in range(CT):
                            last = pe.matmul(PA[g % ASLOTS][:, :], W[:, c, qk, ot * P:(ot + 1) * P],
                                             XT[i][:, c, ch * CH:(ch + 1) * CH], start=(c == 0), stop=(c == CT - 1))
                        last.then_inc(qk_ready, 1)
                    for t in range(TT):
                        if t >= 2 or i >= 1:
                            pe.wait_ge(v_copied, b * TT + t - 1)
                        for c in range(CT):
                            pe.matmul(PV[t % 2][:, 0:C], XT[i][:, c, t * P:(t + 1) * P], W[:, c, 2, :],
                                      start=(c == 0), stop=False)
                        pe.matmul(PV[t % 2][:, 0:C], ONES[:, :], BV[:, :], start=False, stop=True).then_inc(v_ready, 1)
                if B > 2:
                    pe.wait_ge(qk_read, bb * (2 * G) + 2 * G)
                    pe.wait_ge(v_copied, bb * (2 * TT) + 2 * TT)

        @block.vector
        def _(dve):
            dve.wait_ge(const_in, 16 * 5)
            dve.wait_ge(v_init, 3)
            with dve.Fori(0, B // 2) as bb:
                for i in range(2):
                    b = bb * 2 + i

                    def low_part(g):
                        dve.wait_ge(mid_ready, b * G + g + 1)
                        tile, ch = g // NCH, g % NCH
                        nc.vector.tensor_tensor(S[tile % 2][:, 2, ch * CH:(ch + 1) * CH], R[:, g % 2, :],
                                                S[tile % 2][:, 1, ch * CH:(ch + 1) * CH], ALU.subtract).then_inc(lo_ready, 1)

                    for g in range(G):
                        qk, ot, ch = g // (CT * NCH), (g // NCH) % CT, g % NCH
                        dve.wait_ge(qk_ready, b * G + g + 1)
                        dve.wait_ge(f_ready, b * G + g + 1)
                        nc.vector.scalar_tensor_tensor(T1[:, g % 2, :], PA[g % ASLOTS][:, :], BIAS[:, 2 * qk, ot:ot + 1],
                                                       COS[:, ch * CH:(ch + 1) * CH], ALU.add, ALU.mult)
                        nc.vector.stream_shuffle(T2[:, g % 2, :], PA[g % ASLOTS][:, :], SWAP).then_inc(qk_read, 1)
                        dve.wait_ge(qk_read, b * G + g + 1)
                        nc.vector.scalar_tensor_tensor(T2[:, g % 2, :], T2[:, g % 2, :], BIAS[:, 2 * qk + 1, ot:ot + 1],
                                                       SIN[:, ch * CH:(ch + 1) * CH], ALU.add, ALU.mult).then_inc(rot_ready, 1)
                        if g >= 2:
                            low_part(g - 2)
                    low_part(G - 2)
                    low_part(G - 1)

        @block.scalar
        def _(act):
            act.wait_ge(v_init, 3)
            with act.Fori(0, B // 2) as bb:
                for i in range(2):
                    b = bb * 2 + i
                    def middle_part(g):
                        tile, ch = g // NCH, g % NCH
                        act.wait_ge(r_ready, b * G + g + 1)
                        nc.scalar.copy(S[tile % 2][:, 1, ch * CH:(ch + 1) * CH], R[:, g % 2, :]).then_inc(mid_ready, 1)

                    for g in range(G):
                        tile, ch = g // NCH, g % NCH
                        if ch == 0:
                            if tile >= 2:
                                act.wait_ge(s_out[tile % 2], (b * CT + tile // 2) * 16)
                            elif i == 1:
                                act.wait_ge(s_out[tile % 2], b * CT * 16)
                        act.wait_ge(f_ready, b * G + g + 3)
                        nc.scalar.copy(S[tile % 2][:, 0, ch * CH:(ch + 1) * CH], F[:, g % 2, :]).then_inc(hi_ready, 1)
                        if g >= 1:
                            middle_part(g - 1)
                    middle_part(G - 1)
                    if i == 1:
                        act.wait_ge(v_out, b * 16)
                    for t in range(TT):
                        act.wait_ge(v_ready, b * TT + t + 1)
                        nc.scalar.copy(V[:, :, t, 0:HD], PV[t % 2][:, 0:C].rearrange("p (h f) -> p h f", h=HEADS)).then_inc(v_copied, 1)
                act.wait_ge(v_out, bb * 32 + 32)
                for s in range(2):
                    act.wait_ge(s_out[s], (bb * 2 + 2) * CT * 16)


NB = 4
UNITS = NCH * TT // 2
NCK = TT * NCH
LEAD = 4
PSLOTS = 4
MSLOTS = 3
OUTW = TT // 2 * 32


def full_attention(nc, d):
    ctx = ExitStack()
    with ctx:
        sb, pb, sem = scope(nc, ctx)
        ATT = d["ATT"]
        Q = [sb(f"b_q{i}", [P, T], BF16) for i in range(NB)]
        K = [sb(f"b_k{i}", [P, T], BF16) for i in range(NB)]
        V = [sb(f"b_v{i}", [P, TT, VW], FP32) for i in range(NB)]
        E = sb("b_e", [P, PSLOTS, HALF], FP32)
        MX = sb("b_mx", [P, TT, NCH], FP32)
        NEG = sb("b_neg", [P, 3, TT], FP32)
        NP = sb("b_np", [P, P // TT, TT], BF16)
        MT = sb("b_mt", [PARTS * TT, P], BF16)
        OT = sb("b_ot", [P, T], FP32)
        DEN = sb("b_den", [P, 2, TT // 2, 1], FP32)
        SEL = sb("b_sel", [P, HD + 1], FP32)
        IDB = sb("b_idb", [P, P], BF16)
        PS = [pb(f"b_ps{i}", [P, HALF]) for i in range(2)]
        PO = pb("b_po", [P, CH])
        PM = [pb(f"b_pm{i}", [P, CH]) for i in range(MSLOTS)]
        const_in = sem("b_const_in")
        init = sem("b_init")
        head_in = [sem(f"b_head_in{i}") for i in range(NB)]
        s_ready = sem("b_s_ready")
        e_ready = sem("b_e_ready")
        ring_ready = sem("b_ring_ready")
        ring_read = sem("b_ring_read")
        av_quad = sem("b_av_quad")
        ot_ready = sem("b_ot_ready")
        neg_ready = sem("b_neg_ready")
        m_in = sem("b_m_in")
        link = sem("b_link")
        den_ready = sem("b_den_ready")
        RING = NCK + 2

        def plan():
            uses = []
            for u in range(UNITS):
                now = []
                if u == LEAD + 1:
                    now.append(("out", -1, 1))
                for k in range(2):
                    c = 2 * (u + LEAD) + k
                    now.append(("chunk", 1 + c // NCK, c % NCK))
                if u == UNITS - LEAD:
                    now.append(("turn", 1, 1))
                uses.append(now)
            return uses
        PLAN = plan()

        def steps(first, last, e, peeled):
            for u in range(UNITS):
                yield ("scores", u)
                for place, (kind, dh, k) in enumerate(PLAN[u]):
                    if place == len(PLAN[u]) // 2 and u % 2 == 1 and not (first and e == 0 and u < 2):
                        yield ("values", u // 2 - 1)
                    if peeled and dh > 0 and e + dh >= NB:
                        continue
                    if first and e + dh < 0:
                        continue
                    yield (kind, e + dh, k)
            if last and e == NB - 1:
                yield ("values", UNITS // 2 - 1)
                yield ("out", e, 0)
                yield ("out", e, 1)

        block = ctx.enter_context(nc.Block())
        ITERS = NBH // NB

        def schedule(part):
            out = []
            if part == "first":
                out += [("load", h, 0) for h in range(3)]
                out += [("chunk", 0, c) for c in range(NCK)] + [("turn", 0, 0)]
                out += [("chunk", 1, c) for c in range(2 * LEAD)]
            for e in range(NB):
                if not (part == "last" and e > 0):
                    out.append(("load", e + 3, 0))
                out += [(s[0], e, s[1]) if s[0] in ("scores", "values") else s
                        for s in steps(part == "first", part == "last", e, part == "last")]
            return out
        FIRST, MIDDLE, LAST = schedule("first"), schedule("middle"), schedule("last")

        def count(sched, kinds):
            return sum(1 for s in sched if s[0] in kinds)
        RINGK = ("chunk", "turn", "out")
        assert count(MIDDLE, RINGK) == NB * RING and NB * RING % MSLOTS == 0
        R0 = count(FIRST, RINGK)

        def run(engine, step):
            def pass_over(sched, i, base):
                n = dict(ring=0, scores=0, values=0, par=0)
                n.update(base)
                for s in sched:
                    step(s, i, n)
                    n["par"] = (n["par"] + (s[0] in RINGK)) % MSLOTS
                    key = "ring" if s[0] in RINGK else s[0]
                    n[key] = n.get(key, 0) + 1
                return n
            n0 = pass_over(FIRST, 0, {})
            with engine.Fori(1, ITERS - 1) as i:
                grow = dict(ring=NB * RING, scores=NB * UNITS, values=NB * UNITS // 2)
                base = {k: (i - 1) * g + n0.get(k, 0) for k, g in grow.items()}
                base["par"] = R0 % MSLOTS
                n = pass_over(MIDDLE, i, base)
            last = {k: (ITERS - 2) * g + n0.get(k, 0) for k, g in grow.items()}
            last["par"] = R0 % MSLOTS
            pass_over(LAST, ITERS - 1, last)

        @block.sync
        def _(sp):
            sp.dma_start(SEL[:, :], d["sel17"]).then_inc(const_in, 16)
            sp.dma_start(IDB[:, :], d["ident_bf16"]).then_inc(const_in, 16)

            def step(s, i, n):
                kind, e, k = s
                h = i * NB + e
                if kind == "load":
                    slot = e % NB
                    if not (isinstance(i, int) and i == 0 and e < NB):
                        sp.wait_ge(av_quad, (h - NB + 1) * (UNITS // 2))
                    rows = bass.ds(h * HD, HD)
                    dma = [(Q[slot][0:3 * HD, :], d["qs"][0:3, rows, :]),
                           (Q[slot][3 * HD:5 * HD, :], d["qs"][0:2, rows, :]),
                           (Q[slot][5 * HD:6 * HD, :], d["qs"][0:1, rows, :])]
                    for r, part in enumerate((0, 0, 0, 1, 1, 2)):
                        dma.append((K[slot][r * HD:(r + 1) * HD, :], d["ks"][part:part + 1, rows, :]))
                    for dst, src in dma:
                        sp.dma_start(dst, src).then_inc(head_in[slot], 16)
                    sp.dma_start(V[slot][:, :, :], d["vs"][bass.ds(h, 1), :, :].rearrange("h p (t f) -> p (h t) f", f=VW)).then_inc(head_in[slot], 16)
                elif kind == "turn":
                    sp.wait_ge(ring_read, n["ring"] + 1)
                    for r in range(PARTS):
                        sp.dma_start(Q[e % NB][STACK + r:STACK + r + 1, :], MT[r * TT:(r + 1) * TT, :]).then_inc(m_in, 16)
            run(sp, step)
            sp.wait_ge(m_in, 16 * 3 * NBH)

        LOADS = 10 * 16

        @block.gpsimd
        def _(pool):
            for i in range(NB):
                nc.gpsimd.memset(K[i][STACK:P, :], 1.0).then_inc(init, 1)
            pool.wait_ge(init, NB)
            nc.gpsimd.memset(NP[:, :, :], 0.0).then_inc(init, 1)

        @block.tensor
        def _(pe):
            pe.wait_ge(const_in, 32)
            pe.wait_ge(init, NB + 1)

            def ring_slot(n):
                if not (isinstance(n["ring"], int) and n["ring"] < MSLOTS):
                    pe.wait_ge(ring_read, n["ring"] - MSLOTS + 1)
                return PM[n["par"]]

            def step(s, i, n):
                kind, e, k = s
                h = i * NB + e
                if kind == "scores":
                    quarter, pair = k // (TT // 2), k % (TT // 2)
                    if k == 0:
                        pe.wait_ge(m_in, (h + 1) * 16 * 3)
                    if not (isinstance(i, int) and i == 0 and e == 0 and k < 2):
                        pe.wait_ge(e_ready, n["scores"] - 1)
                    for c in range(2):
                        j = 2 * pair + c
                        last = pe.matmul(PS[k % 2][:, c * CH:(c + 1) * CH], K[e % NB][0:STACK + MROWS, j * P:(j + 1) * P],
                                         Q[e % NB][0:STACK + MROWS, quarter * CH:(quarter + 1) * CH], start=True, stop=True)
                    last.then_inc(s_ready, 1)
                elif kind == "chunk":
                    t, c = k // NCH, k % NCH
                    if k == 0:
                        pe.wait_ge(head_in[e % NB], (i + e // NB + 1) * LOADS)
                    pm = ring_slot(n)
                    pe.matmul(pm[:, :], Q[e % NB][0:STACK, t * P:(t + 1) * P], K[e % NB][0:STACK, c * CH:(c + 1) * CH],
                              start=True, stop=True).then_inc(ring_ready, 1)
                elif kind == "turn":
                    pe.wait_ge(neg_ready, h + 1)
                    pm = ring_slot(n)
                    last = pe.transpose(pm[:, OUTW:OUTW + P // 2].bitcast(BF16),
                                        NP[:, :, :].rearrange("p a t -> p (a t)"), IDB[:, :])
                    if k:
                        last = output(pm, h - 1, 0)
                    last.then_inc(ring_ready, 1)
                elif kind == "values":
                    quarter, quad = k // (TT // 4) % NCH, k % (TT // 4)
                    hv = e if k >= 0 else e - 1
                    pe.wait_ge(e_ready, n["values"] * 2 + 2)
                    if quad == 0 and not (isinstance(i, int) and i == 0 and e == 0 and quarter == 0):
                        pe.wait_ge(ot_ready, (i * NB + hv) * NCH + quarter)
                    for g in range(4):
                        last = pe.matmul(PO[g * VW:(g + 1) * VW, :], V[hv % NB][:, quad * 4 + g, :],
                                         E[:, (2 * k + g // 2) % PSLOTS, g % 2 * CH:(g % 2 + 1) * CH],
                                         start=(quad == 0), stop=(quad == TT // 4 - 1))
                    last.then_inc(av_quad, 1)
                elif kind == "out":
                    pm = ring_slot(n)
                    output(pm, h, k).then_inc(ring_ready, 1)

            def output(pm, h, half):
                pe.wait_ge(ot_ready, (h * 2 + half + 1) * 2)
                for t in range(TT // 2):
                    last = pe.matmul(pm[:, t * 32:t * 32 + HD + 1], OT[:, half * HALF + t * P:half * HALF + (t + 1) * P], SEL[:, :],
                                     start=True, stop=True)
                return last
            run(pe, step)

        @block.scalar
        def _(act):
            def step(s, i, n):
                kind, e, k = s
                if kind == "scores":
                    act.wait_ge(s_ready, n["scores"] + 1)
                    if not (isinstance(i, int) and i == 0 and e == 0 and k < PSLOTS) and k % 2 == 0:
                        act.wait_ge(av_quad, (i * NB + e) * (UNITS // 2) + k // 2 - PSLOTS // 2 + 1)
                    nc.scalar.activation(E[:, k % PSLOTS, :], PS[k % 2][:, :], ACT.Exp, scale=HD ** -0.5).then_inc(e_ready, 1)
            run(act, step)

        @block.vector
        def _(dve):
            dve.wait_ge(init, NB + 1)

            def step(s, i, n):
                kind, e, k = s
                h = i * NB + e
                if kind == "values" and k % (TT // 4) == TT // 4 - 1:
                    quarter = k // (TT // 4) % NCH
                    dve.wait_ge(av_quad, n["values"] + 1)
                    nc.vector.tensor_copy(OT[:, quarter * CH:(quarter + 1) * CH], PO[:, :]).then_inc(ot_ready, 1)
                if kind in RINGK:
                    dve.wait_ge(ring_ready, n["ring"] + 1)
                    pm = PM[n["par"]]
                if kind == "chunk":
                    t, c = k // NCH, k % NCH
                    nc.vector.reduce_max(MX[:, t, c:c + 1], pm[:, :], AX.X).then_inc(ring_read, 1)
                    if k == NCK - 1:
                        dve.wait_ge(ring_read, n["ring"] + 1)
                        nc.vector.tensor_reduce(NEG[:, 0, :], MX[:, :, :], AX.X, ALU.max, negate=True).then_inc(link, 1)
                        dve.wait_ge(link, h * 4 + 1)
                        nc.vector.tensor_copy(NP[:, 0, :], NEG[:, 0, :]).then_inc(link, 1)
                        dve.wait_ge(link, h * 4 + 2)
                        nc.vector.tensor_tensor(NEG[:, 1, :], NEG[:, 0, :], NP[:, 0, :], ALU.subtract).then_inc(link, 1)
                        dve.wait_ge(link, h * 4 + 3)
                        nc.vector.tensor_copy(NP[:, 1, :], NEG[:, 1, :]).then_inc(link, 1)
                        dve.wait_ge(link, h * 4 + 4)
                        nc.vector.tensor_tensor(NP[:, 2, :], NEG[:, 1, :], NP[:, 1, :], ALU.subtract).then_inc(neg_ready, 1)
                elif kind == "turn":
                    if not (isinstance(i, int) and i == 0 and e == 0):
                        dve.wait_ge(m_in, h * 16 * 3)
                    last = nc.vector.tensor_copy(MT[:, :], pm[:, OUTW:OUTW + P // 2].bitcast(BF16)[0:PARTS * TT, :])
                    if k:
                        last = output(pm, h - 1, 0)
                    last.then_inc(ring_read, 1)
                elif kind == "out":
                    output(pm, h, k).then_inc(ring_read, 1)

            def output(pm, h, half):
                o = pm[:, 0:OUTW].rearrange("p (t f) -> p t f", f=32)
                nc.vector.reciprocal(DEN[:, half, :, :], o[:, :, HD:HD + 1]).then_inc(den_ready, 1)
                dve.wait_ge(den_ready, h * 2 + half + 1)
                return nc.vector.tensor_tensor(ATT[:, bass.ds(h * TT + half * (TT // 2), TT // 2), :], o[:, :, 0:HD],
                                               DEN[:, half, :, :].to_broadcast([P, TT // 2, HD]), ALU.mult)
            run(dve, step)


EPS = 1e-5
DH = 8
DD = 64
ROT = 32
TOP = T // 8
NEGBIG = -1e30


def first_norm(nc, d):
    ctx = ExitStack()
    with ctx:
        sb, pb, sem = scope(nc, ctx)
        ATT = d["ATT"][:, :, :].rearrange("p (n t) f -> p n t f", t=TT)
        X1T = d["X1T"]
        WO = sb("c_wo", [P, CT, C], FP32)
        BO = sb("c_bo", [1, C], FP32)
        ONES = sb("c_ones", [1, P], FP32)
        IDF = sb("c_idf", [P, P], FP32)
        WV = sb("c_wv", [P, CT, DH * DD], FP32)
        XB = sb("c_x", [P, TT, C], FP32)
        STG = [sb(f"c_stg{i}", [P, C], FP32) for i in range(2)]
        AT = [sb(f"c_at{i}", [P, CT, P], FP32) for i in range(2)]
        ST = sb("c_st", [P, TT, 6], FP32)
        MV = sb("c_mv", [P, TT, 2], FP32)
        STD = sb("c_std", [P, TT], FP32)
        MARK = sb("c_mark", [P, 1], FP32)
        RSTD = sb("c_rstd", [P, TT], FP32)
        VD = [sb(f"c_vd{i}", [P, DH * DD], FP32) for i in range(2)]
        PT = [pb(f"c_pt{i}", [P, CT, P]) for i in range(2)]
        PY = [pb(f"c_py{i}", [P, C]) for i in range(2)]
        PV = [pb(f"c_pv{i}", [P, DH * DD]) for i in range(2)]
        const_in = sem("c_const_in")
        ones_set = sem("c_ones_set")
        x_in = sem("c_x_in")
        staged = sem("c_staged")
        turned = sem("c_turned")
        copied = sem("c_copied")
        y_ready = sem("c_y_ready")
        sum_ready = sem("c_sum_ready")
        stat_ready = sem("c_stat_ready")
        aggr_ready = sem("c_aggr_ready")
        var_ready = sem("c_var_ready")
        std_ready = sem("c_std_ready")
        rstd_ready = sem("c_rstd_ready")
        norm_ready = sem("c_norm_ready")
        x1t_ready = sem("c_x1t_ready")
        vd_ready = sem("c_vd_ready")
        vd_copied = sem("c_vd_copied")
        vd_out = [sem(f"c_vd_out{i}") for i in range(2)]
        x1_out = sem("c_x1_out")
        block = ctx.enter_context(nc.Block())

        @block.sync
        def _(sp):
            sp.dma_start(WO[:, :, :], d["woT"].rearrange("(c p) o -> p c o", p=P)).then_inc(const_in, 16)
            sp.dma_start(BO[:, :], d["bo"]).then_inc(const_in, 16)
            sp.dma_start(IDF[:, :], d["ident"]).then_inc(const_in, 16)
            sp.dma_start(WV[:, :, :], d["wdv"].rearrange("(c p) o -> p c o", p=P)).then_inc(const_in, 16)

            def load_x(b):
                sp.dma_start(XB[:, :, :], d["x"][bass.ds(b, 1), :, :].rearrange("b (t p) c -> p (b t) c", p=P)).then_inc(x_in, 16)

            def stores(b):
                for t in range(TT):
                    sp.wait_ge(vd_copied, b * TT + t + 1)
                    sp.dma_start(d["vd"][bass.ds(b * DH, DH), :, t, :].rearrange("n p f -> p n f"),
                                 VD[t % 2][:, :].rearrange("p (n f) -> p n f", n=DH)).then_inc(vd_out[t % 2], 16)
                sp.wait_ge(norm_ready, b * TT + TT)
                for name in ("x1", "y"):
                    sp.dma_start(d[name][bass.ds(b * T, T), :].rearrange("(t p) c -> p t c", p=P), XB[:, :, :]).then_inc(x1_out, 16)
            load_x(0)
            with sp.Fori(0, B - 1) as b:
                stores(b)
                sp.wait_ge(x1_out, b * 32 + 32)
                load_x(b + 1)
            stores(B - 1)
            sp.wait_ge(x1_out, B * 32)
            for i in range(2):
                sp.wait_ge(vd_out[i], 16 * B * TT // 2)

        @block.gpsimd
        def _(pool):
            nc.gpsimd.memset(ONES[:, :], 1.0).then_inc(ones_set, 1)
            with pool.Fori(0, B) as b:
                for t in range(TT):
                    if t >= 2:
                        pool.wait_ge(turned, b * 2 * TT + t - 1)
                    nc.gpsimd.tensor_copy(STG[t % 2][:, :].rearrange("p (n f) -> p n f", f=HD),
                                          ATT[:, bass.ds(b * HEADS, HEADS), t, :]).then_inc(staged, 1)
                for t in range(TT):
                    pool.wait_ge(copied, b * 2 * TT + TT + t + 1)
                    nc.gpsimd.tensor_copy(X1T[:, :, bass.ds(b * T + t * P, P)], AT[t % 2][:, :, :]).then_inc(x1t_ready, 1)

        @block.tensor
        def _(pe):
            pe.wait_ge(const_in, 64)
            pe.wait_ge(ones_set, 1)
            with pe.Fori(0, B) as b:
                def project(t):
                    pe.wait_ge(copied, b * 2 * TT + t + 1)
                    if t >= 2:
                        pe.wait_ge(sum_ready, b * TT + t - 1)
                    for c in range(CT):
                        pe.matmul(PY[t % 2][:, :], AT[t % 2][:, c, :], WO[:, c, :], start=(c == 0), stop=False)
                    pe.matmul(PY[t % 2][:, :], ONES[:, :], BO[:, :], start=False, stop=True).then_inc(y_ready, 1)
                for t in range(TT):
                    pe.wait_ge(staged, b * TT + t + 1)
                    if t >= 2:
                        pe.wait_ge(copied, b * 2 * TT + t - 1)
                    for c in range(CT):
                        last = pe.transpose(PT[t % 2][:, c, :], STG[t % 2][:, c * P:(c + 1) * P], IDF[:, :])
                    last.then_inc(turned, 1)
                    if t >= 1:
                        project(t - 1)
                project(TT - 1)

                def values(t):
                    pe.wait_ge(copied, b * 2 * TT + TT + t + 1)
                    if t >= 2:
                        pe.wait_ge(vd_copied, b * TT + t - 1)
                    for c in range(CT):
                        last = pe.matmul(PV[t % 2][:, :], AT[t % 2][:, c, :], WV[:, c, :], start=(c == 0), stop=(c == CT - 1))
                    last.then_inc(vd_ready, 1)
                for t in range(TT):
                    pe.wait_ge(norm_ready, b * TT + t + 1)
                    pe.wait_ge(copied, b * 2 * TT + TT + t - 1)
                    for c in range(CT):
                        last = pe.transpose(PT[t % 2][:, c, :], XB[:, t, c * P:(c + 1) * P], IDF[:, :])
                    last.then_inc(turned, 1)
                    if t >= 1:
                        values(t - 1)
                values(TT - 1)
                pe.wait_ge(vd_copied, b * TT + TT)

        @block.scalar
        def _(act):
            with act.Fori(0, B) as b:
                for t in range(TT):
                    act.wait_ge(turned, b * 2 * TT + t + 1)
                    if t >= 2:
                        act.wait_ge(y_ready, b * TT + t - 1)
                    nc.scalar.copy(AT[t % 2][:, :, :], PT[t % 2][:, :, :]).then_inc(copied, 1)
                act.wait_ge(var_ready, b + 1)
                nc.scalar.activation(STD[:, :], STD[:, :], ACT.Sqrt).then_inc(std_ready, 1)

                def values(t):
                    act.wait_ge(vd_ready, b * TT + t + 1)
                    if t >= 2:
                        act.wait_ge(vd_out[t % 2], (b * (TT // 2) + t // 2) * 16)
                    nc.scalar.copy(VD[t % 2][:, :], PV[t % 2][:, :]).then_inc(vd_copied, 1)
                act.wait_ge(y_ready, b * TT + TT)
                for t in range(TT):
                    act.wait_ge(turned, b * 2 * TT + TT + t + 1)
                    if t >= 2:
                        act.wait_ge(x1t_ready, b * TT + t - 1)
                        act.wait_ge(vd_ready, b * TT + t - 1)
                    nc.scalar.copy(AT[t % 2][:, :, :], PT[t % 2][:, :, :]).then_inc(copied, 1)
                    if t >= 1:
                        values(t - 1)
                values(TT - 1)
                act.wait_ge(x1t_ready, b * TT + TT)
                for i in range(2):
                    act.wait_ge(vd_out[i], (b + 1) * (TT // 2) * 16)

        @block.vector
        def _(dve):
            with dve.Fori(0, B) as b:
                dve.wait_ge(x_in, b * 16 + 16)
                for t in range(TT):
                    dve.wait_ge(y_ready, b * TT + t + 1)
                    nc.vector.tensor_tensor(XB[:, t, :], PY[t % 2][:, :], XB[:, t, :], ALU.add).then_inc(sum_ready, 1)
                    if t >= 1:
                        dve.wait_ge(sum_ready, b * TT + t)
                        nc.vector.bn_stats(ST[:, t - 1, :], XB[:, t - 1, :]).then_inc(stat_ready, 1)
                dve.wait_ge(sum_ready, b * TT + TT)
                nc.vector.bn_stats(ST[:, TT - 1, :], XB[:, TT - 1, :]).then_inc(stat_ready, 1)
                dve.wait_ge(stat_ready, b * TT + TT)
                nc.vector.memset(MARK[:, :], 0.0)
                for t in range(TT):
                    last = nc.vector.bn_aggr(MV[:, t, :], ST[:, t, :])
                last.then_inc(aggr_ready, 1)
                dve.wait_ge(aggr_ready, b + 1)
                nc.vector.tensor_scalar(STD[:, :], MV[:, :, 1], EPS, None, ALU.add).then_inc(var_ready, 1)
                dve.wait_ge(std_ready, b + 1)
                nc.vector.reciprocal(RSTD[:, :], STD[:, :]).then_inc(rstd_ready, 1)
                dve.wait_ge(rstd_ready, b + 1)
                for t in range(TT):
                    nc.vector.tensor_scalar(XB[:, t, :], XB[:, t, :], MV[:, t, 0:1], RSTD[:, t:t + 1],
                                            ALU.subtract, ALU.mult).then_inc(norm_ready, 1)


def top_tokens(nc, d):
    ctx = ExitStack()
    with ctx:
        sb, pb, sem = scope(nc, ctx)
        X1T, VAL, IDX = d["X1T"], d["VAL"], d["IDX"]
        R = B * DH
        RW = sb("t_rw", [P, CT, B, R], FP32)
        SC = sb("t_sc", [R, T], FP32)
        V8 = sb("t_v8", [R, 8], FP32)
        I8 = sb("t_i8", [R, 8], U32)
        PS = pb("t_ps", [R, T])
        rw_in = sem("t_rw_in")
        score_ready = sem("t_score_ready")
        step = sem("t_step")
        max_ready = sem("t_max_ready")
        taken = sem("t_taken")
        idx_ready = sem("t_idx_ready")
        block = ctx.enter_context(nc.Block())

        @block.sync
        def _(sp):
            sp.dma_start(RW[:, :, :, :], d["router"].rearrange("(c p) b r -> p c b r", p=P)).then_inc(rw_in, 16)

        @block.tensor
        def _(pe):
            pe.wait_ge(rw_in, 16)
            for ch in range(NCH):
                for b in range(B):
                    for c in range(CT):
                        last = pe.matmul(PS[:, ch * CH:(ch + 1) * CH], RW[:, c, b, :],
                                         X1T[:, c, b * T + ch * CH:b * T + (ch + 1) * CH],
                                         start=(b == 0 and c == 0), stop=(b == B - 1 and c == CT - 1))
                last.then_inc(score_ready, 1)

        @block.vector
        def _(dve):
            for ch in range(NCH):
                dve.wait_ge(score_ready, ch + 1)
                nc.vector.tensor_copy(SC[:, ch * CH:(ch + 1) * CH], PS[:, ch * CH:(ch + 1) * CH]).then_inc(step, 1)
            dve.wait_ge(step, NCH)
            with dve.Fori(0, TOP // 8) as k:
                eight = bass.ds(k * 8, 8)
                nc.vector.max(V8[:, :], SC[:, :]).then_inc(max_ready, 1)
                dve.wait_ge(max_ready, k + 1)
                nc.vector.tensor_scalar(VAL[:, eight], V8[:, :], 0.0, None, ALU.add)
                nc.vector.max_index(I8[:, :], V8[:, :], SC[:, :])
                nc.vector.match_replace(SC[:, :], V8[:, :], SC[:, :], -3.0e38).then_inc(taken, 1)
                dve.wait_ge(taken, k + 1)
                nc.vector.tensor_scalar(IDX[:, eight], I8[:, :], 0.0, None, ALU.add).then_inc(idx_ready, 1)
            dve.wait_ge(idx_ready, TOP // 8)


def routed_branch(nc, d):
    ctx = ExitStack()
    with ctx:
        sb, pb, sem = scope(nc, ctx)
        VAL, IDX = d["VAL"], d["IDX"]
        R = B * DH
        KT = TOP // P
        IDF = sb("m_idf", [P, P], FP32)
        ROW0 = sb("m_row0", [P, R], FP32)
        GATE = sb("m_gate", [R, TOP], FP32)
        IG = sb("m_ig", [P, 2, KT, R], FP32)
        OFFF = sb("m_offf", [P, KT, R], FP32)
        OFFX = [sb(f"m_offx{i}", [P, KT], U32) for i in range(2)]
        OFFP = [sb(f"m_offp{i}", [P, KT], U32) for i in range(2)]
        OFFS = [sb(f"m_offs{i}", [P, KT], U32) for i in range(2)]
        POSG = [sb(f"m_posg{i}", [P, 2, KT], FP32) for i in range(2)]
        XG = [sb(f"m_xg{i}", [P, KT, C], FP32) for i in range(2)]
        CS = [sb(f"m_cs{i}", [P, KT, 2 * ROT], FP32) for i in range(2)]
        WM = [sb(f"m_wm{i}", [P, CT, 3 * DD], FP32) for i in range(2)]
        WO = [sb(f"m_wo{i}", [DD, C], FP32) for i in range(2)]
        KEYP = [sb(f"m_keyp{i}", [P, TOP], FP32) for i in range(2)]
        XGT = [sb(f"m_xgt{i}", [P, CT, TOP], FP32) for i in range(2)]
        T1 = [sb(f"m_t1{i}", [P, KT, 2, ROT], FP32) for i in range(2)]
        T2 = [sb(f"m_t2{i}", [P, KT, 2, ROT], FP32) for i in range(2)]
        QKR = [sb(f"m_qkr{i}", [P, KT, 2, DD], FP32) for i in range(2)]
        VS = [sb(f"m_vs{i}", [P, KT, DD], FP32) for i in range(2)]
        QKT = [sb(f"m_qkt{i}", [DD, 2, TOP], FP32) for i in range(2)]
        MASK = [sb(f"m_mask{i}", [P, KT, TOP], FP32) for i in range(2)]
        SS = [sb(f"m_ss{i}", [P, KT, TOP], FP32) for i in range(2)]
        NM = [sb(f"m_nm{i}", [P, 2, KT], FP32) for i in range(2)]
        DEN = [sb(f"m_den{i}", [P, 3, KT], FP32) for i in range(2)]
        PR = [sb(f"m_pr{i}", [P, KT, TOP], FP32) for i in range(2)]
        PRT = [sb(f"m_prt{i}", [P, KT, TOP], FP32) for i in range(2)]
        AV = [sb(f"m_av{i}", [DD, TOP], FP32) for i in range(2)]
        Y = [sb(f"m_y{i}", [P, KT, C], FP32) for i in range(2)]
        BANK = [[pb(f"m_bank{i}_{n}", [P, CH]) for n in range(3)] for i in range(2)]

        def view(bank, rows, a):
            return [BANK[i][bank][0:rows, :].rearrange("p (a f) -> p a f", a=a) for i in range(2)]
        PX, PS, PY = view(0, P, CT), view(0, P, KT), view(0, P, KT)
        PQ, PP = view(1, P, KT), view(1, P, KT)
        PQT = view(2, DD, 2)
        PA = [BANK[i][2][0:DD, 0:TOP] for i in range(2)]
        gate_exp = sem("m_gate_exp")
        link = sem("m_link")
        gate_ready = sem("m_gate_ready")
        turned = sem("m_turned")
        idx_out = sem("m_idx_out")
        off_ready = sem("m_off_ready")
        go = sem("m_go")
        gathered = [sem(f"m_gathered{i}") for i in range(2)]
        w_in = [sem(f"m_w_in{i}") for i in range(2)]
        wo_in = [sem(f"m_wo_in{i}") for i in range(2)]
        xt_ready = sem("m_xt_ready")
        xt_copied = sem("m_xt_copied")
        qkv_ready = sem("m_qkv_ready")
        rot_mul = sem("m_rot_mul")
        rot_ready = sem("m_rot_ready")
        v_copied = sem("m_v_copied")
        qkt_ready = sem("m_qkt_ready")
        qkt_copied = sem("m_qkt_copied")
        s_ready = sem("m_s_ready")
        mask_ready = sem("m_mask_ready")
        ss_ready = sem("m_ss_ready")
        nm_ready = sem("m_nm_ready")
        bias_ready = sem("m_bias_ready")
        p_ready = sem("m_p_ready")
        pt_ready = sem("m_pt_ready")
        pt_copied = sem("m_pt_copied")
        av_ready = sem("m_av_ready")
        av_copied = sem("m_av_copied")
        den_ready = sem("m_den_ready")
        gd_ready = sem("m_gd_ready")
        py_ready = sem("m_py_ready")
        px_free = sem("m_px_free")
        y_ready = sem("m_y_ready")
        added = sem("m_added")
        block = ctx.enter_context(nc.Block())
        PAIRS = DH // 2

        def loop(eng, stages):
            with eng.Fori(0, R // 2) as k:
                for stage in stages:
                    for i in range(2):
                        stage(i, k, k * 2 + i)

        def ahead(eng, body):
            with eng.Fori(0, R // 2 - 1) as k:
                body(k, True)
            body(R // 2 - 1, False)

        @block.sync
        def _(sp):
            sp.dma_start(d["idxd"], IDX[:, :]).then_inc(idx_out, 16)
            sp.wait_ge(idx_out, 16)

            def keys_and_weights(i, h, n):
                sp.dma_start(WM[i][:, :, :], d["wm"][bass.ds(n, 1), :, :].rearrange("n (c p) f -> p (n c) f", p=P)).then_inc(w_in[i], 16)
                sp.dma_start(KEYP[i][:, :], d["idxd"][bass.ds(h, 1), :].to_broadcast([P, TOP])).then_inc(w_in[i], 16)

            def output_weights(i, n):
                sp.dma_start(WO[i][:, :], d["wmo"][bass.ds(n * DD, DD), :]).then_inc(wo_in[i], 16)

            def pair(b, pr):
                for i in range(2):
                    h, n = b * DH + pr * 2 + i, pr * 2 + i
                    sp.wait_ge(qkv_ready, h + 1)
                    sp.wait_ge(mask_ready, h + 1)
                    keys_and_weights(i, h + 2, n + 2)
                for i in range(2):
                    sp.wait_ge(py_ready, b * DH + pr * 2 + i + 1)
                    output_weights(i, pr * 2 + i + 2)
            for i in range(2):
                keys_and_weights(i, i, i)
                output_weights(i, i)
            with sp.Fori(0, B - 1) as b:
                with sp.Fori(0, PAIRS) as pr:
                    pair(b, pr)
            with sp.Fori(0, PAIRS - 1) as pr:
                pair(B - 1, pr)

        @block.gpsimd
        def _(pool):
            for dst, name in ((IDF, "ident"), (ROW0, "row0")):
                half = dst.shape[1] // 2
                for part in (slice(0, half), slice(half, 2 * half)):
                    pool.dma_start(dst[:, part], d[name][:, part]).then_inc(added, 16)

            def gather(i, h):
                pool.wait_ge(off_ready, h + 1)
                pool.sem_inc(go, 1)
                for t in range(KT):
                    pool.indirect_dma_start(out=XG[i][:, t, :], out_offset=None, in_=d["x1"],
                                            in_offset=bass.IndirectOffsetOnAxis(ap=OFFX[i][:, t:t + 1], axis=0)).then_inc(gathered[i], 16)
                    pool.indirect_dma_start(out=CS[i][:, t, :], out_offset=None, in_=d["cs64"],
                                            in_offset=bass.IndirectOffsetOnAxis(ap=OFFP[i][:, t:t + 1], axis=0)).then_inc(gathered[i], 16)

            def scatter(i, h):
                pool.wait_ge(y_ready, h + 1)
                pool.wait_ge(added, h * 32 + 64)
                pool.sem_inc(go, 1)
                for t in range(KT):
                    pool.indirect_dma_start(out=d["y"], out_offset=bass.IndirectOffsetOnAxis(ap=OFFS[i][:, t:t + 1], axis=0),
                                            in_=Y[i][:, t, :], in_offset=None, compute_op=ALU.add).then_inc(added, 16)

            def body(k, more):
                if more:
                    for i in range(2):
                        gather(i, k * 2 + 2 + i)
                for i in range(2):
                    scatter(i, k * 2 + i)
            for i in range(2):
                gather(i, i)
            ahead(pool, body)
            pool.wait_ge(added, 32 * R + 64)

        @block.tensor
        def _(pe):
            pe.wait_ge(added, 64)
            for t in range(KT):
                pe.matmul(PX[0][:, 0, t * R:(t + 1) * R], IDX[:, t * P:(t + 1) * P], IDF[0:R, 0:R], start=True, stop=True)
            pe.wait_ge(gate_ready, 1)
            for t in range(KT):
                last = pe.matmul(PX[0][:, 0, (KT + t) * R:(KT + t + 1) * R], GATE[:, t * P:(t + 1) * P], IDF[0:R, 0:R],
                                 start=True, stop=True)
            last.then_inc(turned, 1)
            pe.wait_ge(link, 4)

            pe.sem_inc(px_free, 2)

            def turn_rows(i, k, h):
                pe.wait_ge(gathered[i], k * 64 + 64)
                pe.wait_ge(px_free, h + 1)
                for c in range(CT):
                    for t in range(KT):
                        last = pe.transpose(PX[i][:, c, t * P:(t + 1) * P], XG[i][:, t, c * P:(c + 1) * P], IDF[:, :])
                last.then_inc(xt_ready, 1)

            def project(i, k, h):
                pe.wait_ge(w_in[i], k * 32 + 32)
                pe.wait_ge(xt_copied, h + 1)
                for t in range(KT):
                    for c in range(CT):
                        last = pe.matmul(PQ[i][:, t, 0:3 * DD], XGT[i][:, c, t * P:(t + 1) * P], WM[i][:, c, :],
                                         start=(c == 0), stop=(c == CT - 1))
                last.then_inc(qkv_ready, 1)

            def turn_qk(i, k, h):
                pe.wait_ge(rot_ready, h + 1)
                pe.wait_ge(v_copied, h + 1)
                for q in range(2):
                    for t in range(KT):
                        last = pe.matmul(PQT[i][:, q, t * P:(t + 1) * P], QKR[i][:, t, q, :], IDF[:, :], start=True, stop=True)
                last.then_inc(qkt_ready, 1)

            def scores(i, k, h):
                pe.wait_ge(qkt_copied, h + 1)
                for t in range(KT):
                    last = pe.matmul(PS[i][:, t, :], QKT[i][:, 0, t * P:(t + 1) * P], QKT[i][:, 1, :], start=True, stop=True)
                last.then_inc(s_ready, 1)

            def turn_probabilities(i, k, h):
                pe.wait_ge(p_ready, h + 1)
                for kt in range(KT):
                    for t in range(KT):
                        last = pe.transpose(PP[i][:, kt, t * P:(t + 1) * P], PR[i][:, t, kt * P:(kt + 1) * P], IDF[:, :])
                last.then_inc(pt_ready, 1)

            def values(i, k, h):
                pe.wait_ge(pt_copied, h + 1)
                for kt in range(KT):
                    last = pe.matmul(PA[i], VS[i][:, kt, :], PRT[i][:, kt, :], start=(kt == 0), stop=(kt == KT - 1))
                last.then_inc(av_ready, 1)

            def output(i, k, h):
                pe.wait_ge(av_copied, h + 1)
                pe.wait_ge(wo_in[i], k * 16 + 16)
                for t in range(KT):
                    last = pe.matmul(PY[i][:, t, :], AV[i][:, t * P:(t + 1) * P], WO[i][:, :], start=True, stop=True)
                last.then_inc(py_ready, 1)
            loop(pe, [turn_rows, project, turn_qk, scores, turn_probabilities, values, output])

        @block.scalar
        def _(act):
            nc.scalar.activation(GATE[:, :], VAL[:, :], ACT.Exp, scale=-1.0).then_inc(gate_exp, 1)

            def rows(i, k, h):
                act.wait_ge(xt_ready, h + 1)
                nc.scalar.copy(XGT[i][:, :, :], PX[i]).then_inc(xt_copied, 1)

            def values(i, k, h):
                act.wait_ge(qkv_ready, h + 1)
                nc.scalar.copy(QKR[i][:, :, :, ROT:DD], PQ[i][:, :, 0:2 * DD].rearrange("p t (q f) -> p t q f", q=2)[:, :, :, ROT:DD])
                nc.scalar.copy(VS[i][:, :, :], PQ[i][:, :, 2 * DD:3 * DD]).then_inc(v_copied, 1)

            def queries_keys(i, k, h):
                act.wait_ge(qkt_ready, h + 1)
                nc.scalar.copy(QKT[i][:, :, :], PQT[i]).then_inc(qkt_copied, 1)

            def exponentials(i, k, h):
                act.wait_ge(bias_ready, h + 1)
                for t in range(KT):
                    last = nc.scalar.activation(PR[i][:, t, :], SS[i][:, t, :], ACT.Exp, bias=NM[i][:, 1, t:t + 1], scale=DD ** -0.5,
                                                accum_out=DEN[i][:, 0, t:t + 1])
                last.then_inc(p_ready, 1)

            def probabilities(i, k, h):
                act.wait_ge(pt_ready, h + 1)
                nc.scalar.copy(PRT[i][:, :, :], PP[i]).then_inc(pt_copied, 1)

            def outputs(i, k, h):
                act.wait_ge(av_ready, h + 1)
                nc.scalar.copy(AV[i][:, :], PA[i]).then_inc(av_copied, 1)
            loop(act, [rows, values, queries_keys, exponentials, probabilities, outputs])

        @block.vector
        def _(dve):
            dve.wait_ge(gate_exp, 1)
            nc.vector.tensor_scalar(GATE[:, :], GATE[:, :], 1.0, None, ALU.add).then_inc(link, 1)
            dve.wait_ge(link, 1)
            nc.vector.reciprocal(GATE[:, :], GATE[:, :]).then_inc(gate_ready, 1)
            dve.wait_ge(turned, 1)
            nc.vector.tensor_copy(IG[:, :, :, :].rearrange("p a t r -> p (a t r)"), PX[0].rearrange("p a f -> p (a f)")[:, 0:2 * KT * R]).then_inc(link, 1)
            dve.wait_ge(link, 2)
            dve.wait_ge(added, 64)
            nc.vector.tensor_tensor(OFFF[:, :, :], IG[:, 0, :, :], ROW0[:, :].unsqueeze(1).to_broadcast([P, KT, R]), ALU.add).then_inc(link, 1)
            dve.wait_ge(link, 3)
            nc.vector.memset(NM[0][:, :, :], 0.0).then_inc(link, 1)

            def offsets(i, h):
                row = bass.ds(h, 1)
                nc.vector.tensor_scalar(OFFX[i][:, :].unsqueeze(2), OFFF[:, :, row], 0.0, None, ALU.add)
                nc.vector.tensor_scalar(POSG[i][:, :, :].unsqueeze(3), IG[:, :, :, row], 0.0, None, ALU.add)
                nc.vector.tensor_scalar(OFFP[i][:, :].unsqueeze(2), IG[:, 0, :, row], 0.0, None, ALU.add).then_inc(off_ready, 1)
            for i in range(2):
                offsets(i, i)

            def mask(i, k, h):
                dve.wait_ge(w_in[i], k * 32 + 32)
                dve.wait_ge(off_ready, h + 1)
                for t in range(KT):
                    last = nc.vector.tensor_scalar(MASK[i][:, t, :], KEYP[i][:, :], POSG[i][:, 0, t:t + 1], NEGBIG, ALU.is_gt, ALU.mult)
                last.then_inc(mask_ready, 1)

            def rotation_terms(i, k, h):
                dve.wait_ge(v_copied, h + 1)
                dve.wait_ge(gathered[i], k * 64 + 64)
                X = PQ[i][:, :, 0:2 * DD].rearrange("p t (q f) -> p t q f", q=2)
                H = ROT // 2

                def table(a, b):
                    return CS[i][:, :, a:b].unsqueeze(2).to_broadcast([P, KT, 2, b - a])
                nc.vector.tensor_tensor(T1[i][:, :, :, :], X[:, :, :, 0:ROT], table(0, ROT), ALU.mult)
                nc.vector.tensor_tensor(T2[i][:, :, :, 0:H], X[:, :, :, H:ROT], table(ROT, ROT + H), ALU.mult)
                nc.vector.tensor_tensor(T2[i][:, :, :, H:ROT], X[:, :, :, 0:H], table(ROT + H, 2 * ROT), ALU.mult).then_inc(rot_mul, 1)
                dve.wait_ge(rot_mul, h + 1)
                nc.vector.tensor_tensor(QKR[i][:, :, :, 0:ROT], T1[i][:, :, :, :], T2[i][:, :, :, :], ALU.add).then_inc(rot_ready, 1)

            def maxima(i, k, h):
                dve.wait_ge(s_ready, h + 1)
                dve.wait_ge(mask_ready, h + 1)
                nc.vector.tensor_tensor(SS[i][:, :, :], PS[i], MASK[i][:, :, :], ALU.add).then_inc(ss_ready, 1)
                dve.wait_ge(ss_ready, h + 1)
                nc.vector.tensor_reduce(NM[i][:, 0, :], SS[i][:, :, :], AX.X, ALU.max, negate=True).then_inc(nm_ready, 1)
                dve.wait_ge(nm_ready, h + 1)
                nc.vector.tensor_scalar(NM[i][:, 1, :], NM[i][:, 0, :], DD ** -0.5, None, ALU.mult).then_inc(bias_ready, 1)

            def gates(i, k, h):
                dve.wait_ge(p_ready, h + 1)
                nc.vector.reciprocal(DEN[i][:, 1, :], DEN[i][:, 0, :]).then_inc(den_ready, 1)
                dve.wait_ge(den_ready, h + 1)
                nc.vector.tensor_tensor(DEN[i][:, 2, :].unsqueeze(2), DEN[i][:, 1, :].unsqueeze(2), IG[:, 1, :, bass.ds(h, 1)],
                                        ALU.mult).then_inc(gd_ready, 1)

            def outputs(i, k, h):
                dve.wait_ge(added, h * 32 + 32)
                nc.vector.tensor_scalar(OFFS[i][:, :].unsqueeze(2), OFFF[:, :, bass.ds(h, 1)], 0.0, None, ALU.add)
                dve.wait_ge(gd_ready, h + 1)
                dve.wait_ge(py_ready, h + 1)
                for t in range(KT):
                    last = nc.vector.tensor_scalar(Y[i][:, t, :], PY[i][:, t, :], DEN[i][:, 2, t:t + 1], None, ALU.mult)
                last.then_inc(y_ready, 1)
                dve.wait_ge(y_ready, h + 1)
                dve.sem_inc(px_free, 1)

            def body(k, more):
                def both(stage):
                    for i in range(2):
                        stage(i, k, k * 2 + i)
                both(mask)
                both(rotation_terms)
                if more:
                    for i in range(2):
                        offsets(i, k * 2 + 2 + i)
                both(maxima)
                both(gates)
                both(outputs)
            ahead(dve, body)


PIECES = 4
GROUP = 4
ESLOTS = 3
DUNITS = TT // 2 + TT


def dense_branch(nc, d, out):
    ctx = ExitStack()
    with ctx:
        sb, pb, sem = scope(nc, ctx)
        X1T = d["X1T"]
        COS = sb("d_cos", [P, T], FP32)
        SIN = sb("d_sin", [P, T], FP32)
        IDF = sb("d_idf", [P, P], FP32)
        IDB = sb("d_idb", [P, P], BF16)
        NEGQ = sb("d_negq", [P, P], BF16)
        NEGK = sb("d_negk", [P, P], BF16)
        WO = sb("d_wo", [P, DH * DD // P, C], FP32)
        W = [sb(f"d_w{i}", [P, CT, 2 * DD], FP32) for i in range(2)]
        Q = [sb(f"d_q{i}", [DD + 1, T], FP32) for i in range(2)]
        K = [sb(f"d_k{i}", [DD + 1, T], FP32) for i in range(2)]
        KK = sb("d_kk", [P, T], FP32)
        V = [sb(f"d_v{i}", [P, TT, DD], FP32) for i in range(2)]
        QH = sb("d_qh", [P, T], BF16)
        KS = sb("d_ks", [P, T], BF16)
        MP = sb("d_mp", [P, T], BF16)
        ESUM = sb("d_esum", [P, HALF], FP32)
        ONES = sb("d_ones", [P, P], FP32)
        ZERO = sb("d_zero", [P, P], FP32)
        E = sb("d_e", [P, ESLOTS, HALF], FP32)
        AV = sb("d_av", [P, DH // 2, T], FP32)
        RD = sb("d_rd", [P, HALF], FP32)
        T1 = sb("d_t1", [P, CH], FP32)
        T2 = sb("d_t2", [P, CH], FP32)
        MX = sb("d_mx", [P, TT, NCH], FP32)
        NEG = sb("d_neg", [P, P], FP32)
        MT = sb("d_mt", [TT, P], FP32)
        ST = sb("d_st", [P, TT, 6], FP32)
        MV = sb("d_mv", [P, TT, 4], FP32)
        POW = sb("d_pow", [P, GROUP, 1], FP32)
        MARK = sb("d_mark", [P, 1], FP32)
        PS = [pb(f"d_ps{i}", [P, HALF]) for i in range(2)]
        PO = pb("d_po", [P, HALF])
        PM = [pb(f"d_pm{i}", [P, CH]) for i in range(2)]
        const_in = sem("d_const_in")
        init = sem("d_init")
        w_in = [sem(f"d_w_in{i}") for i in range(2)]
        v_in = [sem(f"d_v_in{i}") for i in range(2)]
        k_in = [sem(f"d_k_in{i}") for i in range(2)]
        m_in = sem("d_m_in")
        y_in = sem("d_y_in")
        y_out = sem("d_y_out")
        ring_ready = sem("d_ring_ready")
        ring_read = sem("d_ring_read")
        rot_ready = sem("d_rot_ready")
        qk_sum = sem("d_qk_sum")
        high_ready = sem("d_high_ready")
        next_ready = sem("d_next_ready")
        neg_ready = sem("d_neg_ready")
        s_ready = sem("d_s_ready")
        e_ready = sem("d_e_ready")
        av_ready = sem("d_av_ready")
        esum_ready = sem("d_esum_ready")
        esum_used = sem("d_esum_used")
        esum_go = sem("d_esum_go")
        av_raw = sem("d_av_raw")
        av_part = sem("d_av_part")
        rd_ready = sem("d_rd_ready")
        inv_ready = sem("d_inv_ready")
        rd_go = sem("d_rd_go")
        av_out = sem("d_av_out")
        st_ready = sem("d_st_ready")
        aggr_ready = sem("d_aggr_ready")
        var_ready = sem("d_var_ready")
        std_ready = sem("d_std_ready")
        o_ready = sem("d_o_ready")
        init2 = sem("d_init2")
        CHUNKS = sum(t // NCH + 1 for t in range(TT))
        AHEAD = NCH + CHUNKS + 1
        SUMS = 2 * HALF // CH
        RING = AHEAD + SUMS
        SWAP = [(lane + ROT // 2) % ROT for lane in range(32)]

        def unit(u):
            half, j = (0, u) if u < TT // 2 else (1, u - TT // 2)
            return half, j, max(0, j * P - half * HALF)

        def pieces(x0):
            return [(a, b) for a, b in ((x0, CH), (max(x0, CH), HALF)) if a < b]

        def ahead(e):
            todo = [("product", e, 0)]
            for ch in range(1, NCH):
                todo += [("product", e, ch), ("split", e, ch - 1)]
            todo += [("split", e, NCH - 1), ("keys", e, 0)]
            for t in range(TT):
                todo += [("chunk", e, t * NCH + c) for c in range(t // NCH + 1)]
            todo.append(("turn", e, 0))
            return todo
        RINGK = ("product", "chunk", "turn", "out", "sum")
        PROJECTED, WAITED, CHUNKED, TURNED = 7, 9, DUNITS - 5, DUNITS - 4

        def due(todo, u):
            keys, turn = 2 * NCH + 1, len(todo) - 1
            if u <= PROJECTED:
                return keys * u // PROJECTED
            if u <= CHUNKED:
                return keys + max(0, (turn - keys) * (u - WAITED) // (CHUNKED - WAITED))
            return turn if u < TURNED else len(todo)

        def pair_steps(more, closing=False):
            out = []
            for e in range(2):
                todo = ahead(e + 1) if e == 0 or more else []
                if e == 0 or more:
                    out.append(("values_in", e + 1, 0))
                if e == 1 and closing:
                    out.append(("y_in", 0, 0))
                if more:
                    out.append(("weights_in", e + 2, 0))
                done = 0
                for u in range(DUNITS):
                    out.append(("scores", e, u))
                    if TT // 2 < u <= TT // 2 + PIECES:
                        out.append(("inverse", e, u - TT // 2 - 1))
                    want = due(todo, u) if todo else 0
                    middle = (done + want) // 2 if u % 2 == 0 else want
                    out += todo[done:middle]
                    if u == TT // 2:
                        out += [("sum", e, 0), ("sum", e, 1)]
                    if u % 2 == 0 and u >= 2:
                        out.append(("values", e, u // 2 - 1))
                    out += todo[middle:want]
                    done = want
                out += [("values", e, DUNITS // 2 - 1), ("sum", e, 2), ("sum", e, 3)]
                out += [("inverse", e, PIECES + piece) for piece in range(PIECES)]
            return out

        def run(engine, step):
            def walk(steps, b, pr, ring, h):
                n = dict(ring=ring, scores=h * DUNITS, values=h * (DUNITS // 2), halves=h * 2, par=1, b=b, pr=pr, h=h)
                for s in steps:
                    step(s, n)
                    if s[0] in RINGK:
                        n["par"] ^= 1
                        n["ring"] = n["ring"] + 1
                    elif s[0] in ("scores", "values"):
                        n[s[0]] = n[s[0]] + 1
                    if s[0] == "inverse" and s[2] % PIECES == PIECES - 1:
                        n["halves"] = n["halves"] + 1

            def ring_at(b, pr):
                return b * (DH * RING + TT) + pr * (2 * RING) + AHEAD

            def batch(b, last):
                with engine.Fori(0, DH // 2 - 1) as pr:
                    walk(pair_steps(True), b, pr, ring_at(b, pr), b * DH + pr * 2)
                pr = DH // 2 - 1
                walk(pair_steps(not last, True), b, pr, ring_at(b, pr), b * DH + pr * 2)
                ring = ring_at(b, pr) + (RING + SUMS if last else 2 * RING)
                n = dict(ring=ring, par=0 if last else 1, b=b, pr=DH // 2, h=b * DH + DH)
                for t in range(TT):
                    step(("out", 0, t), n)
                    n["par"] ^= 1
                    n["ring"] = n["ring"] + 1
                step(("out_end", 0, TT), n)
            n = dict(ring=0, halves=0, par=0, b=0, pr=0, h=0)
            for s in [("values_in", 0, 0), ("weights_in", 0, 0), ("weights_in", 1, 0)] + ahead(0):
                step(s, n)
                if s[0] in RINGK:
                    n["par"] ^= 1
                    n["ring"] += 1
            assert n["ring"] == AHEAD and AHEAD % 2 == 1 and SUMS % 2 == 0
            with engine.Fori(0, B - 1) as b:
                batch(b, False)
            batch(B - 1, True)

        INIT = 5
        block = ctx.enter_context(nc.Block())

        @block.sync
        def _(sp):
            for dst, name in ((COS, "cos64"), (SIN, "sin64"), (IDF, "ident"), (IDB, "ident_bf16"), (NEGQ, "negq"), (NEGK, "negk")):
                sp.dma_start(dst[:, :], d[name]).then_inc(const_in, 16)
            sp.dma_start(WO[:, :, :], d["wdo"].rearrange("(k p) c -> p k c", p=P)).then_inc(const_in, 16)
            sp.wait_ge(init, INIT)

            def step(s, n):
                kind, e, k = s
                h, b = n["h"], n["b"]
                if kind == "weights_in":
                    sp.dma_start(W[e % 2][:, :, :], d["wd"][bass.ds(n["pr"] * 2 + e, 1), :, :]
                                 .rearrange("n (c p) f -> p (n c) f", p=P)).then_inc(w_in[e % 2], 16)
                elif kind == "values_in":
                    if n.get("scores") is not None:
                        sp.wait_ge(av_ready, (h + e - 1) * (DUNITS // 2) + 2)
                    sp.dma_start(V[e % 2][:, :, :], d["vd"][bass.ds(h + e, 1), :, :, :]
                                 .rearrange("n p t f -> p (n t) f")).then_inc(v_in[e % 2], 16)
                elif kind == "keys":
                    sp.wait_ge(qk_sum, (h + e + 1) * NCH + 2)
                    sp.dma_start(K[e % 2][0:DD, :], KK[DD:P, :]).then_inc(k_in[e % 2], 16)
                    sp.wait_ge(high_ready, (h + e + 1) * NCH)
                    sp.dma_start(QH[DD:P, :], QH[0:DD, :]).then_inc(k_in[e % 2], 16)
                    sp.dma_start(KS[0:DD, :], MP[DD:P, :]).then_inc(k_in[e % 2], 16)
                elif kind == "turn":
                    sp.wait_ge(ring_read, n["ring"] + 3)
                    sp.dma_start(Q[e % 2][DD:DD + 1, :], MT[:, :]).then_inc(m_in, 16)
                elif kind == "y_in":
                    sp.wait_ge(qk_sum, (h + 2) * NCH + 2)
                    for c in range(CT):
                        sp.dma_start(X1T[:, c, bass.ds(b * T, T)].rearrange("p (t c) -> p t c", c=C),
                                     d["y"][bass.ds(b * T + c * HALF, HALF), :].rearrange("(t p) c -> p t c", p=P)).then_inc(y_in, 16)
                elif kind == "out" and k % GROUP == 0 and k > GROUP:
                    store(b, k // GROUP - 2)
                elif kind == "out_end":
                    for g in (TT // GROUP - 2, TT // GROUP - 1):
                        store(b, g)

            def store(b, g):
                sp.wait_ge(o_ready, b * TT + (g + 1) * GROUP)
                c, t = g * GROUP // (TT // CT), g * GROUP % (TT // CT)
                sp.dma_start(out[bass.ds(b, 1), g * GROUP * P:(g + 1) * GROUP * P, :].rearrange("b (t p) c -> p (b t) c", p=P),
                             X1T[:, c, bass.ds(b * T + t * C, GROUP * C)].rearrange("p (t c) -> p t c", c=C)).then_inc(y_out, 16)
            run(sp, step)
            sp.wait_ge(y_out, B * TT // GROUP * 16)

        @block.gpsimd
        def _(pool):
            for n, (dst, value) in enumerate(((K[0][DD:DD + 1, :], 1.0), (K[1][DD:DD + 1, :], 1.0), (ONES[:, :], 1.0),
                                              (ZERO[:, :], 0.0), (POW[:, :, :], -0.5))):
                nc.gpsimd.memset(dst, value).then_inc(init, 1)
                pool.wait_ge(init, n + 1)
            pool.sem_inc(av_out, 1)
            pool.sem_inc(esum_ready, ESLOTS)
            pool.sem_inc(m_in, 16)
            for t in range(2):
                pool.sem_inc(k_in[t], 16)

            def alone(n):
                if n.get("scores") is not None:
                    pool.wait_ge(esum_ready, n["scores"] + ESLOTS)
                pool.wait_ge(av_out, n["halves"] + 1)

            def step(s, n):
                kind, e, k = s
                h = n["h"]
                if kind == "scores":
                    half, j, x0 = unit(k)
                    pool.wait_ge(e_ready, n["scores"] + 3)
                    alone(n)
                    if j == 0:
                        pool.wait_ge(esum_used, (h + e) * 2 + half + 1)
                        pool.sem_inc(esum_go, 1)
                        nc.gpsimd.tensor_tensor(ESUM[:, :], E[:, k % ESLOTS, :], ZERO[:, 0:1].to_broadcast([P, HALF]), ALU.add).then_inc(esum_ready, 1)
                    else:
                        nc.gpsimd.tensor_tensor(ESUM[:, x0:HALF], ESUM[:, x0:HALF], E[:, k % ESLOTS, x0:HALF], ALU.add).then_inc(esum_ready, 1)
                elif kind == "inverse" and k % PIECES == PIECES - 1:
                    half = k // PIECES
                    pool.wait_ge(av_raw, (h + e) * 2 + half + 2)
                    pool.wait_ge(inv_ready, (h + e) * 2 + half + 1)
                    alone(n)
                    pool.sem_inc(rd_go, 1)
                    mine = slice(e * DD, (e + 1) * DD)
                    part = AV[mine, bass.ds(n["pr"], 1), half * HALF:(half + 1) * HALF]
                    nc.gpsimd.tensor_tensor(part, part, RD[mine, :].unsqueeze(1), ALU.mult).then_inc(av_out, 1)
                elif kind == "out" and k % GROUP == GROUP - 1:
                    pool.wait_ge(var_ready, n["b"] * (TT // GROUP) + k // GROUP + 1)
                    group = MV[:, k - GROUP + 1:k + 1, :]
                    nc.gpsimd.tensor_tensor(group[:, :, 3:4], group[:, :, 2:3], POW[:, :, :], ALU.pow).then_inc(std_ready, 1)

            run(pool, step)

        @block.tensor
        def _(pe):
            pe.wait_ge(const_in, 16 * 7)
            pe.wait_ge(init, INIT)
            pe.sem_inc(av_ready, 2)
            pe.sem_inc(esum_used, 1)

            def step(s, n):
                kind, e, k = s
                h, b, pr = n["h"], n["b"], n["pr"]
                h2 = b * (DH // 2) + pr
                if kind in RINGK:
                    pe.wait_ge(ring_read, n["ring"] + 1)
                    pm = PM[n["par"]]
                if kind == "product":
                    if k == 0:
                        pe.wait_ge(w_in[e % 2], (h2 + e // 2 + 1) * 16)
                    ch = k
                    bb = b + 1 if isinstance(pr, int) and pr == DH // 2 - 1 and e == 2 else b
                    for c in range(CT):
                        last = pe.matmul(pm[:, :], W[e % 2][:, c, :], X1T[:, c, bass.ds(bb * T + ch * CH, CH)],
                                         start=(c == 0), stop=(c == CT - 1))
                    last.then_inc(ring_ready, 1)
                elif kind == "chunk":
                    t, c = k // NCH, k % NCH
                    if t == 0:
                        pe.wait_ge(next_ready, (h + e + 1) * NCH)
                        pe.wait_ge(k_in[e % 2], (h2 + e // 2 + 1) * 48 + 16)
                    w = min(CH, (t + 1) * P - c * CH)
                    diag = c == t // NCH
                    pe.matmul(pm[:, 0:w], QH[:, t * P:(t + 1) * P], KS[:, c * CH:c * CH + w], start=True, stop=False)
                    last = pe.matmul(pm[:, 0:w], MP[0:DD, t * P:(t + 1) * P], KS[0:DD, c * CH:c * CH + w],
                                     start=False, stop=not diag)
                    if diag:
                        last = pe.matmul(pm[:, w - P:w], IDB[:, :], NEGQ[:, :], start=False, stop=True)
                    last.then_inc(ring_ready, 1)
                elif kind == "turn":
                    pe.wait_ge(neg_ready, h + e + 1)
                    pe.transpose(pm[:, 0:P], NEG[:, :], IDF[:, :]).then_inc(ring_ready, 1)
                elif kind == "scores":
                    half, j, x0 = unit(k)
                    if k == 0:
                        pe.wait_ge(m_in, (h + e + 1) * 16 + 16)
                    pe.wait_ge(e_ready, n["scores"] + 1)
                    diag = j * P >= half * HALF
                    for a, z in pieces(x0):
                        own = diag and a == x0
                        last = pe.matmul(PS[k % 2][:, a:z], K[e][:, j * P:(j + 1) * P], Q[e][:, half * HALF + a:half * HALF + z],
                                         start=True, stop=not own)
                        if own:
                            last = pe.matmul(PS[k % 2][:, x0:x0 + P], IDB[:, :], NEGK[:, :], start=False, stop=True)
                    last.then_inc(s_ready, 1)
                elif kind == "values":
                    half = 0 if 2 * k < TT // 2 else 1
                    pair = k - half * (TT // 4)
                    if k == 0:
                        pe.wait_ge(v_in[e], (h2 + 1) * 16)
                    pe.wait_ge(e_ready, n["values"] * 2 + 4)
                    if pair == 0:
                        pe.wait_ge(av_raw, (h + e) * 2 + half + 1)
                    for bank in range(HALF // CH):
                        for odd in range(2):
                            _, j, x0 = unit(2 * k + odd)
                            rows = slice(odd * DD, (odd + 1) * DD)
                            end = (half * HALF + (bank + 1) * CH) // P - 2 + odd
                            a, z = max(x0, bank * CH), (bank + 1) * CH
                            if pair == 0 and a > bank * CH and odd:
                                last = pe.matmul(PO[rows, 0:a], V[e][:, j, :], ZERO[:, 0:a], start=True, stop=True)
                            if a < z:
                                last = pe.matmul(PO[rows, a:z], V[e][:, j, :], E[:, (2 * k + odd) % ESLOTS, a:z],
                                                 start=(pair == 0), stop=(j == end))
                    last.then_inc(av_ready, 1)
                elif kind == "sum":
                    half, c = k // 2, k % 2
                    pe.wait_ge(esum_ready, (h + e) * DUNITS + (TT // 2 if half == 0 else DUNITS) + ESLOTS)
                    last = pe.matmul(pm[:, :], ONES[:, :], ESUM[:, c * CH:(c + 1) * CH], start=True, stop=True)
                    last.then_inc(ring_ready, 1)
                    if c == 1:
                        pe.wait_ge(ring_ready, n["ring"] + 1)
                        pe.sem_inc(esum_used, 1)
                elif kind == "out":
                    if k == 0:
                        pe.wait_ge(av_out, h * 2 + 1)
                    for kt in range(DH // 2):
                        last = pe.matmul(pm[:, 0:C], AV[:, kt, k * P:(k + 1) * P], WO[:, kt, :],
                                         start=(kt == 0), stop=(kt == DH // 2 - 1))
                    last.then_inc(ring_ready, 1)
            run(pe, step)

        @block.scalar
        def _(act):
            act.sem_inc(e_ready, 2)

            def step(s, n):
                kind, e, k = s
                if kind == "scores":
                    _, _, x0 = unit(k)
                    act.wait_ge(s_ready, n["scores"] + 1)
                    act.wait_ge(av_ready, (n["h"] + e) * (DUNITS // 2) + k // 2 + 1 + k % 2)
                    act.wait_ge(esum_ready, n["scores"] + 1)
                    nc.scalar.activation(E[:, k % ESLOTS, x0:HALF], PS[k % 2][:, x0:HALF], ACT.Exp,
                                         scale=DD ** -0.5).then_inc(e_ready, 1)
                elif kind == "split":
                    cols = slice(k * CH, (k + 1) * CH)
                    act.wait_ge(qk_sum, (n["h"] + e) * NCH + k + 3)
                    nc.scalar.copy(QH[0:DD, cols], Q[e % 2][0:DD, cols])
                    nc.scalar.copy(MP[DD:P, cols], KK[DD:P, cols]).then_inc(high_ready, 1)
            run(act, step)

        @block.vector
        def _(dve):
            nc.vector.memset(MX[:, :, :], -3.0e38).then_inc(init2, 1)
            nc.vector.memset(NEG[:, :], 0.0).then_inc(init2, 1)
            dve.sem_inc(ring_read, 2)
            dve.sem_inc(av_raw, 1)
            dve.sem_inc(qk_sum, 2)
            dve.wait_ge(const_in, 16 * 7)
            dve.wait_ge(init2, 2)

            def step(s, n):
                kind, e, k = s
                h, b, pr = n["h"], n["b"], n["pr"]
                if kind in RINGK:
                    dve.wait_ge(ring_ready, n["ring"] + 1)
                    pm = PM[n["par"]]
                if kind == "product":
                    ch, g = k, (h + e) * NCH + k
                    dve.wait_ge(qk_sum, g + 2)
                    nc.vector.tensor_tensor(T1[:, :], pm[:, :], COS[:, ch * CH:(ch + 1) * CH], ALU.mult)
                    nc.vector.stream_shuffle(T2[:, :], pm[:, :], SWAP).then_inc(ring_read, 1)
                    dve.wait_ge(ring_read, n["ring"] + 3)
                    nc.vector.tensor_tensor(T2[:, :], T2[:, :], SIN[:, ch * CH:(ch + 1) * CH], ALU.mult).then_inc(rot_ready, 1)
                    if ch == 0 and e >= 1:
                        dve.wait_ge(av_ready, (h + e - 1) * (DUNITS // 2) + 2)
                        dve.wait_ge(k_in[(e + 1) % 2], (b * (DH // 2) + pr + 1) * 48 + 16)
                    dve.wait_ge(rot_ready, g + 1)
                    cols = slice(ch * CH, (ch + 1) * CH)
                    nc.vector.tensor_tensor(Q[e % 2][0:DD, cols], T1[0:DD, :], T2[0:DD, :], ALU.add)
                    nc.vector.tensor_tensor(KK[DD:P, cols], T1[DD:P, :], T2[DD:P, :], ALU.add).then_inc(qk_sum, 1)
                elif kind == "split":
                    cols = slice(k * CH, (k + 1) * CH)
                    dve.wait_ge(high_ready, (h + e) * NCH + k + 1)
                    nc.vector.tensor_tensor(MP[0:DD, cols], Q[e % 2][0:DD, cols], QH[0:DD, cols], ALU.subtract)
                    nc.vector.tensor_tensor(KS[DD:P, cols], KK[DD:P, cols], MP[DD:P, cols], ALU.subtract).then_inc(next_ready, 1)
                elif kind == "sum":
                    half, c = k // 2, k % 2
                    dve.wait_ge(av_out, (h + e) * 2 + half + 1)
                    mine = slice(e * DD, (e + 1) * DD)
                    nc.vector.tensor_copy(RD[mine, c * CH:(c + 1) * CH], pm[mine, :]).then_inc(ring_read, 1)
                    if c == 1:
                        dve.wait_ge(ring_read, n["ring"] + 3)
                        dve.sem_inc(rd_ready, 1)
                elif kind == "chunk":
                    t, c = k // NCH, k % NCH
                    w = min(CH, (t + 1) * P - c * CH)
                    nc.vector.reduce_max(MX[:, t, c:c + 1], pm[:, 0:w], AX.X).then_inc(ring_read, 1)
                    if k == TT * NCH - 1:
                        dve.wait_ge(ring_read, n["ring"] + 3)
                        nc.vector.tensor_reduce(NEG[:, 0:TT], MX[:, :, :], AX.X, ALU.max, negate=True).then_inc(neg_ready, 1)
                elif kind == "turn":
                    dve.wait_ge(m_in, (h + e) * 16 + 16)
                    nc.vector.tensor_copy(MT[:, :], pm[0:TT, 0:P]).then_inc(ring_read, 1)
                elif kind == "values":
                    half = 0 if 2 * k < TT // 2 else 1
                    if k in (TT // 4 - 1, DUNITS // 2 - 1):
                        dve.wait_ge(av_ready, n["values"] + 3)
                        mine = slice(e * DD, (e + 1) * DD)
                        part = AV[mine, bass.ds(pr, 1), half * HALF:(half + 1) * HALF]
                        nc.vector.tensor_copy(part, PO[0:DD, :].unsqueeze(1)).then_inc(av_part, 1)
                        dve.wait_ge(av_part, (h + e) * 2 + half + 1)
                        nc.vector.tensor_tensor(part, PO[DD:P, :].unsqueeze(1), part, ALU.add).then_inc(av_raw, 1)
                elif kind == "inverse":
                    half, piece = k // PIECES, k % PIECES
                    if piece == 0:
                        dve.wait_ge(rd_ready, (h + e) * 2 + half + 1)
                    part = RD[e * DD:(e + 1) * DD, piece * HALF // PIECES:(piece + 1) * HALF // PIECES]
                    last = nc.vector.reciprocal(part, part)
                    if piece == PIECES - 1:
                        last.then_inc(inv_ready, 1)
                elif kind == "out":
                    if k == 0:
                        dve.wait_ge(y_in, (b + 1) * 32)
                    nc.vector.tensor_tensor(tile(b, k), pm[:, 0:C], tile(b, k), ALU.add).then_inc(ring_read, 1)
                    if k > GROUP:
                        norm(b, k - GROUP - 1)
                    dve.wait_ge(ring_read, n["ring"] + 3)
                    nc.vector.memset(MARK[:, :], 0.0)
                    nc.vector.bn_stats(ST[:, k, :], tile(b, k)).then_inc(st_ready, 1)
                    if k % GROUP == GROUP - 1:
                        dve.wait_ge(st_ready, b * TT + k + 1)
                        nc.vector.memset(MARK[:, :], 0.0)
                        for t in range(k - GROUP + 1, k + 1):
                            last = nc.vector.bn_aggr(MV[:, t, 0:2], ST[:, t, :])
                        last.then_inc(aggr_ready, 1)
                        dve.wait_ge(aggr_ready, b * (TT // GROUP) + k // GROUP + 1)
                        group = MV[:, k - GROUP + 1:k + 1, :]
                        nc.vector.tensor_scalar(group[:, :, 2:3], group[:, :, 1:2], EPS, None, ALU.add).then_inc(var_ready, 1)
                elif kind == "out_end":
                    for t in range(TT - GROUP - 1, TT):
                        norm(b, t)

            def tile(b, t):
                return X1T[:, t // (TT // CT), bass.ds(b * T + t % (TT // CT) * C, C)]

            def norm(b, t):
                dve.wait_ge(std_ready, b * (TT // GROUP) + t // GROUP + 1)
                nc.vector.tensor_scalar(tile(b, t), tile(b, t), MV[:, t, 0:1], MV[:, t, 3:4],
                                        ALU.subtract, ALU.mult).then_inc(o_ready, 1)
            run(dve, step)


def kernel_program(nc, d, out):
    with nc.sbuf_tensor("x1t", [P, CT, B * T], FP32) as X1T:
        d["X1T"] = X1T
        project_attention(nc, d)
        with nc.sbuf_tensor("att", [P, NBH * TT, HD], FP32) as ATT:
            d["ATT"] = ATT
            full_attention(nc, d)
            first_norm(nc, d)
        with (nc.sbuf_tensor("val", [B * DH, TOP], FP32) as VAL, nc.sbuf_tensor("idx", [B * DH, TOP], FP32) as IDX):
            d.update(VAL=VAL, IDX=IDX)
            top_tokens(nc, d)
            routed_branch(nc, d)
        dense_branch(nc, d, out)


def swap_halves(a, width, half):
    import numpy as np
    heads = a.reshape((-1, width) + a.shape[1:])
    parts = [heads[:, half:2 * half], heads[:, 0:half], heads[:, 2 * half:]]
    return np.concatenate(parts, axis=1).reshape(a.shape)


def rotation(inv, length, width):
    import numpy as np
    half = len(inv)
    ang = (np.arange(length, dtype=np.float32)[None, :] * inv[:, None]).astype(np.float32)
    cos, sin = np.cos(ang).astype(np.float32), np.sin(ang).astype(np.float32)
    rest = width - 2 * half
    c = np.concatenate([cos, cos, np.ones((rest, length), np.float32)])
    s = np.concatenate([-sin, sin, np.zeros((rest, length), np.float32)])
    return c, s


def kernel(**inputs):
    import numpy as np
    import ml_dtypes
    import concourse.bacc as bacc
    from concourse.bass_utils import run_bass_kernel_spmd
    nc = bacc.Bacc("TRN2", target_bir_lowering=False, num_devices=1)
    x = np.asarray(inputs["L0_attn_x"])
    W = {k: np.asarray(inputs["L0_attn_W" + k]) for k in "qkvo"}
    bias = {k: np.asarray(inputs["L0_attn_b" + k]) for k in "qkvo"}

    def swapped(a):
        return swap_halves(a, HD, HD // 2)
    bcol = [bias["q"], swapped(bias["q"]), bias["k"], swapped(bias["k"])]
    base = np.float32(10000.0)
    cos16, sin16 = rotation(1.0 / base ** (np.arange(0, HD, 2, dtype=np.float32) / HD), T, HD)
    cos32, sin32 = rotation(base ** (-np.arange(ROT // 2, dtype=np.float32) / (ROT // 2)), T, DD)
    sel = np.zeros((P, HD + 1), np.float32)
    for g in range(4):
        for f in range(HD + 1):
            sel[g * VW + f, f] = 1.0
    router = np.asarray(inputs["L0_ffn_mosa_router_w"])
    routed = np.zeros((C, B, B * DH), np.float32)
    for b in range(B):
        routed[:, b, b * DH:(b + 1) * DH] = router
    wd = np.asarray(inputs["L0_ffn_dense_wqkv"])
    plain = [wd[:, :, 0:DD], wd[:, :, DD:2 * DD]]
    wd4 = np.concatenate(plain, axis=2).transpose(1, 0, 2)
    wd4 = np.concatenate([wd4, wd4[0:2]], axis=0)
    wm = np.asarray(inputs["L0_ffn_mosa_wqkv"]).transpose(1, 0, 2)
    wmo = np.asarray(inputs["L0_ffn_mosa_wo"])
    after = np.triu(np.full((P, P), NEGBIG, np.float32), 1)
    arrays = {
        "x": x,
        "xT": x.transpose(0, 2, 1),
        "wqkv": np.stack([W[k].T for k in "qkv"], axis=1),
        "bqk": np.stack(bcol).reshape(4, CT, P).transpose(2, 0, 1),
        "bv": bias["v"][None, :],
        "cos16": np.tile(cos16, (P // HD, 1)),
        "sin16": np.tile(sin16, (P // HD, 1)),
        "sel17": sel,
        "woT": W["o"].T,
        "bo": bias["o"][None, :],
        "ident": np.eye(P, dtype=np.float32),
        "wdv": np.asarray(inputs["L0_ffn_dense_wqkv"])[:, :, 2 * DD:].reshape(C, DH * DD),
        "wd": wd4,
        "wdo": np.asarray(inputs["L0_ffn_dense_wo"]),
        "cos64": np.tile(cos32, (2, 1)),
        "sin64": np.tile(sin32, (2, 1)),
        "negq": after.astype(ml_dtypes.bfloat16),
        "negk": after.T.astype(ml_dtypes.bfloat16),
        "router": routed,
        "row0": np.broadcast_to((np.arange(B * DH) // DH * T).astype(np.float32), (P, B * DH)),
        "cs64": np.concatenate([cos32[:ROT].T, sin32[:ROT].T], axis=1),
        "wm": np.concatenate([wm, wm[0:2]]),
        "wmo": np.concatenate([wmo, wmo[0:2 * DD]]),
        "ident_bf16": np.eye(P).astype(ml_dtypes.bfloat16),
    }
    arrays = {k: np.ascontiguousarray(v) for k, v in arrays.items()}
    d = {k: nc.dram_tensor("in_" + k, v.shape, mybir.dt.from_np(v.dtype), kind="ExternalInput").ap() for k, v in arrays.items()}
    for name, shape, dt in (("qs", (PARTS, B * C, T), BF16), ("ks", (PARTS, B * C, T), BF16), ("vs", (NBH, P, TT * VW), FP32),
                            ("idxd", (B * DH, TOP), FP32), ("x1", (B * T, C), FP32), ("y", (B * T, C), FP32), ("vd", (B * DH, P, TT, DD), FP32)):
        d[name] = nc.dram_tensor("scratch_" + name, shape, dt).ap()
    out = nc.dram_tensor("out", (B, T, C), FP32, kind="ExternalOutput").ap()
    kernel_program(nc, d, out)
    got = run_bass_kernel_spmd(nc, [{"in_" + k: v for k, v in arrays.items()}], core_ids=[0])
    return got.results[0]["out"]
```
